# Optimizing a Trainium2 kernel written in Bass

```python
import numpy as np
import jax
import jax.numpy as jnp

def _softmax(x, axis=-1):
    return jax.nn.softmax(x, axis=axis)

def _gelu(x):
    return jax.nn.gelu(x, approximate=True)

def _silu(x):
    return jax.nn.silu(x)

def _sigmoid(x):
    return jax.nn.sigmoid(x)

def _layernorm(x, axis=-1, eps=1e-05):
    m = jnp.mean(x, axis=axis, keepdims=True)
    v = jnp.var(x, axis=axis, keepdims=True)
    return (x - m) / jnp.sqrt(v + eps)

def _scatter_add(tgt, idx, src, axis=0):
    return tgt.at[idx].add(src)

def _segment_sum(src, seg, n):
    return jax.ops.segment_sum(src, seg, n)
kernel_name = 'mk_seq_postln_d1_jaxref_r4_ce4fcf'

def setup_inputs(seed: int=0):
    np.random.seed(seed)
    _w = jnp.asarray

    def _L0_attn_setup():
        import jax, jax.numpy as jnp
        import numpy as np
        B, N, D = (2, 512, 256)
        H, FD, HD = (16, 16, 64)
        ENC = 128
        EPS = 1e-12
        RD = 4.0
        RRD = 2.0
        R2 = float(np.sqrt(2.0))

        def taylor_exp(x):
            x2 = (x[..., :, None] * x[..., None, :]).reshape(*x.shape[:-1], FD * FD) / R2
            return jnp.concatenate([jnp.ones_like(x[..., :1]), x / RRD, x2 / RD], axis=-1)
        key = jax.random.key(seed)
        ks = jax.random.split(key, 7)
        s = 1.0 / np.sqrt(D)
        x = jax.random.normal(ks[0], (B, N, D), dtype=jnp.float32)
        Wq = jax.random.normal(ks[1], (H * FD, D), dtype=jnp.float32) * s
        Wk = jax.random.normal(ks[2], (H * FD, D), dtype=jnp.float32) * s
        Wv = jax.random.normal(ks[3], (H * HD, D), dtype=jnp.float32) * s
        Wk_enc = jax.random.normal(ks[4], (H * FD, D), dtype=jnp.float32) * s
        Wv_enc = jax.random.normal(ks[5], (H * HD, D), dtype=jnp.float32) * s
        Wout = jax.random.normal(ks[6], (D, H * HD), dtype=jnp.float32) * s
        return {'x': x, 'Wq': Wq, 'Wk': Wk, 'Wv': Wv, 'Wk_enc': Wk_enc, 'Wv_enc': Wv_enc, 'Wout': Wout}
    _L0_attn_in = _L0_attn_setup()

    def _L0_ffn_setup():
        import jax, jax.numpy as jnp
        import numpy as np
        E, H, I = (8, 256, 1024)
        B, S = (4, 512)
        key = jax.random.key(seed)
        k0, k1, k2, k3 = jax.random.split(key, 4)
        s = 0.02
        return {'hidden_states': jax.random.normal(k0, (B, S, H), dtype=jnp.float32), 'w1': jax.random.normal(k1, (E, H, I), dtype=jnp.float32) * s, 'b1': jnp.zeros((E, I), dtype=jnp.float32), 'w2': jax.random.normal(k2, (E, I, H), dtype=jnp.float32) * s, 'b2': jnp.zeros((E, H), dtype=jnp.float32), 'wr': jax.random.normal(k3, (H, E), dtype=jnp.float32) * s, 'br': jnp.zeros((E,), dtype=jnp.float32)}
    _L0_ffn_in = _L0_ffn_setup()
    _d = {'L0_attn_x': _L0_attn_in['x'], 'L0_attn_Wq': _L0_attn_in['Wq'], 'L0_attn_Wk': _L0_attn_in['Wk'], 'L0_attn_Wv': _L0_attn_in['Wv'], 'L0_attn_Wk_enc': _L0_attn_in['Wk_enc'], 'L0_attn_Wv_enc': _L0_attn_in['Wv_enc'], 'L0_attn_Wout': _L0_attn_in['Wout'], 'L0_ffn_w1': _L0_ffn_in['w1'], 'L0_ffn_b1': _L0_ffn_in['b1'], 'L0_ffn_w2': _L0_ffn_in['w2'], 'L0_ffn_b2': _L0_ffn_in['b2'], 'L0_ffn_wr': _L0_ffn_in['wr'], 'L0_ffn_br': _L0_ffn_in['br']}
    _x0 = _d['L0_attn_x']
    _d['L0_attn_x'] = jax.random.normal(jax.random.fold_in(jax.random.key(seed), 1), (8, 512, 256), dtype=_x0.dtype)
    del _x0
    return _d

def reference(L0_attn_x, L0_attn_Wq, L0_attn_Wk, L0_attn_Wv, L0_attn_Wk_enc, L0_attn_Wv_enc, L0_attn_Wout, L0_ffn_w1, L0_ffn_b1, L0_ffn_w2, L0_ffn_b2, L0_ffn_wr, L0_ffn_br):

    def _L0_attn_ref(x, Wq, Wk, Wv, Wk_enc, Wv_enc, Wout):
        import jax, jax.numpy as jnp
        import numpy as np
        B, N, D = (2, 512, 256)
        H, FD, HD = (16, 16, 64)
        ENC = 128
        EPS = 1e-12
        RD = 4.0
        RRD = 2.0
        R2 = float(np.sqrt(2.0))

        def taylor_exp(x):
            x2 = (x[..., :, None] * x[..., None, :]).reshape(*x.shape[:-1], FD * FD) / R2
            return jnp.concatenate([jnp.ones_like(x[..., :1]), x / RRD, x2 / RD], axis=-1)
        b, n, _ = x.shape
        q = (x @ Wq.T).reshape(b, n, H, FD).transpose(0, 2, 1, 3)
        k = (x @ Wk.T).reshape(b, n, H, FD).transpose(0, 2, 1, 3)
        v = (x @ Wv.T).reshape(b, n, H, HD).transpose(0, 2, 1, 3)
        x_enc = x[:, :ENC]
        k_enc = (x_enc @ Wk_enc.T).reshape(b, ENC, H, FD).transpose(0, 2, 1, 3)
        v_enc = (x_enc @ Wv_enc.T).reshape(b, ENC, H, HD).transpose(0, 2, 1, 3)
        k_enc_f = taylor_exp(k_enc)
        q_f = taylor_exp(q)
        k_f = taylor_exp(k)
        A_qk = jnp.einsum('bhnd,bhmd->bhnm', q_f, k_f)
        A_qk = jnp.tril(A_qk)
        y1 = jnp.einsum('bhnm,bhme->bhne', A_qk, v)
        A_qk2 = jnp.einsum('bhnd,bhmd->bhnm', q_f, k_enc_f)
        y2 = jnp.einsum('bhnm,bhme->bhne', A_qk2, v_enc)
        k_state = k_enc_f.sum(axis=2, keepdims=True) + jnp.cumsum(k_f, axis=2)
        z = 1.0 / ((q_f * k_state).sum(axis=-1) + EPS)
        out = (y1 + y2) * z[..., None]
        out = out.transpose(0, 2, 1, 3).reshape(b, n, H * HD)
        return out @ Wout.T

    def _L0_ffn_ref(hidden_states, w1, b1, w2, b2, wr, br):
        import jax, jax.numpy as jnp
        import numpy as np
        E, H, I = (8, 256, 1024)
        B, S = (4, 512)
        b, s, h = hidden_states.shape
        x = hidden_states.reshape(-1, h)
        logits = x @ wr + br
        probs = jax.nn.softmax(logits, axis=-1)
        top_p, top_i = jax.lax.top_k(probs, 2)
        gate = top_p[:, 0] / (top_p[:, 0] + top_p[:, 1])
        top1 = top_i[:, 0]
        out = jnp.zeros_like(x)
        n_experts = w1.shape[0]
        for e in range(n_experts):
            hmid = jax.nn.gelu(x @ w1[e] + b1[e], approximate=False)
            hout = hmid @ w2[e] + b2[e]
            mask = top1 == e
            out = out + jnp.where(mask[:, None], hout * gate[:, None], 0.0)
        return out.reshape(b, s, h)
    x = L0_attn_x
    x = _layernorm(x + _L0_attn_ref(x, L0_attn_Wq, L0_attn_Wk, L0_attn_Wv, L0_attn_Wk_enc, L0_attn_Wv_enc, L0_attn_Wout), axis=-1)
    x = _layernorm(x + _L0_ffn_ref(x, L0_ffn_w1, L0_ffn_b1, L0_ffn_w2, L0_ffn_b2, L0_ffn_wr, L0_ffn_br), axis=-1)
    return x

_drawn_inputs = setup_inputs


def setup_inputs(seed=0):
    import zlib

    import numpy as np

    out = dict(_drawn_inputs(seed))
    spreads = {'L0_ffn_b1': (0.0, 0.409), 'L0_ffn_b2': (0.0, 0.1), 'L0_ffn_br': (0.0, 0.1)}
    factors = {}
    for name, (base, spread) in spreads.items():
        noise = np.random.default_rng([zlib.crc32(name.encode()), seed]).standard_normal(out[name].shape)
        drawn = base * np.exp(spread * noise) if base else spread * noise
        out[name] = jnp.asarray(drawn.astype(out[name].dtype))
    for name, factor in factors.items():
        out[name] = (out[name] * factor).astype(out[name].dtype)
    return out
```

```python
from contextlib import ExitStack

import numpy as np

import concourse.bass as bass
from concourse import mybir

F32 = mybir.dt.float32
F32R = mybir.dt.float32r
BF16 = mybir.dt.bfloat16
I32 = mybir.dt.int32
ALU = mybir.AluOpType
ACT = mybir.ActivationFunctionType
AX = mybir.AxisListType

P = 128
B, N, D = 8, 512, 256
H, FD, HD = 16, 16, 64
NT = N // P
KD = D // P
PAIRS = H // 2
PM = 4
NK = N + P
VP = 3 * HD
E, I = 8, 1024
TOK = B * N
TT = TOK // P
IC = I // P
SLOTS = TT + E - 1
CQ = float(1.0 / (4.0 * np.sqrt(2.0)))
HALF_ROOT = float(np.sqrt(0.5))
EPS_Z, EPS_LN = 1e-12, 1e-5
SKIP = 2 * TOK

BLOCKS = [(NT, 0, 0), (0, 0, 512), (1, 128, 1024), (3, 384, 1408), (2, 256, 1536)]
HALVES = [(0, 1024), (1024, 1792)]
USES = 42
U_Q, U_K, U_KE, U_V, U_YT, U_LG, U_HEAD = 0, 1, 2, 3, 8, 9, 10


def attention_and_experts(nc, xT_in, x_in, wqk_in, wv_in, wo_in, w1_in, b1_in, w2_in, b2_in, wr_in, br_in, out):
    ybuf = nc.dram_tensor("attention_rows", [TOK + 1, D], F32).ap()
    with ExitStack() as ctx:
        def sem(name):
            return ctx.enter_context(nc.semaphore(name))

        logits = ctx.enter_context(nc.sbuf_tensor("logits", [P, TT, E], F32))
        ident = ctx.enter_context(nc.sbuf_tensor("ident", [P, P], F32))
        attention(nc, sem, xT_in, x_in, wqk_in, wv_in, wo_in, wr_in, br_in, ybuf, logits, ident)
        experts(nc, sem, w1_in, b1_in, w2_in, b2_in, ybuf, logits, ident, out)


def attention(nc, sem, xT_in, x_in, wqk_in, wv_in, wo_in, wr_in, br_in, ybuf, logits, ident):
    with ExitStack() as ctx:
        def sb(name, shape, dt=F32):
            return ctx.enter_context(nc.sbuf_tensor(name, shape, dt))

        def ps(name, shape):
            return ctx.enter_context(nc.psum_tensor(name, shape, F32))

        wqk_h, wqk_l = sb("wqk_h", [P, 3, KD, D], F32R), sb("wqk_l", [P, 3, KD, D], F32R)
        wv_h, wv_l = sb("wv_h", [P, 2, KD, I], F32R), sb("wv_l", [P, 2, KD, I], F32R)
        wo = sb("wo", [P, PAIRS, D])
        wr = sb("wr", [P, KD, E])
        br = sb("br", [P, E])
        xT = sb("xT", [P, KD, N])
        xh, xl = sb("xh", [P, KD, N], F32R), sb("xl", [P, KD, N], F32R)
        xrow = sb("xrow", [P, NT, D])
        qh, ql = sb("qh", [P, 2, 2, N], F32R), sb("ql", [P, 2, 2, N], F32R)
        kh, kl = sb("kh", [P, 2, NK], F32R), sb("kl", [P, 2, NK], F32R)
        qop = sb("qop", [P, PM, 2, N], F32R)
        kop = sb("kop", [P, PM, NK], F32R)
        weights = sb("weights", [P, 2, 1792])
        values = sb("values", [P, NT + 1, PAIRS, VP])
        recip = sb("recip", [P, 2, N])
        att = sb("att", [P, 2, N])
        y = sb("y", [P, NT, D])
        yT = sb("yT", [P, NT * KD, P])
        stats = sb("stats", [P, NT, 6])
        mv = sb("mv", [P, NT, 2])
        sdev = sb("sdev", [P, NT])
        rstd = sb("rstd", [P, NT])
        mask = sb("mask", [P, 2, P])
        part_i = sb("part_i", [P, 1], I32)
        odd_i = sb("odd_i", [P, 1], I32)
        cq = sb("cq", [P, 2])
        zrow = sb("zrow", [1, D])

        slot = [ps("slot0", [P, 1024]), ps("slot1", [P, 1024])]
        osum = [ps("osum0", [P, N]), ps("osum1", [P, N])]
        ysum = ps("ysum", [P, NT * D])

        w_loaded = [sem("w_loaded0"), sem("w_loaded1")]
        small_loaded = sem("small_loaded")
        w_split = sem("w_split")
        consts = sem("consts")
        zeroed = sem("zeroed")
        masks = sem("masks")
        cq_ready = sem("cq_ready")
        xT_loaded, xrow_loaded = sem("xT_loaded"), sem("xrow_loaded")
        x_split = sem("x_split")
        slot_full = sem("slot_full")
        slot_free = [sem("slot_free0"), sem("slot_free1")]
        qk_hi, qk_lo = sem("qk_hi"), sem("qk_lo")
        op_ready = [sem(f"op_ready{i}") for i in range(PM)]
        squared, halved, masked = sem("squared"), sem("halved"), sem("masked")
        o_full, d_ready, r_ready, o_free = sem("o_full"), sem("d_ready"), sem("r_ready"), sem("o_free")
        att_used = sem("att_used")
        y_step, sd_ready, y_ready = sem("y_step"), sem("sd_ready"), sem("y_ready")
        yT_ready = sem("yT_ready")
        y_stored = sem("y_stored")
        pool_passed, dve_passed = sem("pool_passed"), sem("dve_passed")

        CHUNKS = [(0, 0), (0, 1), (0, 2), (1, 0), (1, 1), (1, 2), (1, 3)]
        STEPS = 2 + 2 * NT
        FREED = U_HEAD // 2

        def use(it, u):
            if isinstance(it, int) and it == 0:
                return u if u < U_YT else u - 2
            if isinstance(it, int) and it == B:
                return B * USES - 2 + (u - U_YT)
            return it * USES + (u - 2)

        def batches(eng, body):
            body(0, True, False)
            with eng.Fori(1, B - 1) as it:
                body(it, False, False)
            body(B - 1, False, True)

        block = ctx.enter_context(nc.Block())

        @block.sync
        def _(sp):
            sp.dma_start(xT[:, :, :], xT_in[0]).then_inc(xT_loaded, 16)
            for n, (kind, c) in enumerate(CHUNKS):
                if n >= 2:
                    sp.wait_ge(w_split, 2 * (n - 1))
                src = wqk_in[:, c, :] if kind == 0 else wv_in[:, c, :]
                sp.dma_start(weights[:, n % 2, 0:src.shape[1]], src).then_inc(w_loaded[n % 2], 16)
            sp.dma_start(wo[:, :, :], wo_in).then_inc(small_loaded, 16)
            sp.dma_start(wr[:, :, :], wr_in).then_inc(small_loaded, 16)
            sp.dma_start(br[:, :], br_in.partition_broadcast(P)).then_inc(small_loaded, 16)
            sp.wait_ge(zeroed, 1)
            sp.dma_start(ybuf[0:1, :], zrow[:, :]).then_inc(small_loaded, 16)

            def body(it, first, last):
                sp.wait_ge(qk_hi, it * 4 + 4)
                sp.wait_ge(qk_lo, it * 4 + 4)
                for p in range(PAIRS):
                    m, r = p // PM, 32 * (p % PM)
                    if p >= PM:
                        sp.wait_ge(slot_full, use(it, U_HEAD + 4 * (p - PM) + 4))
                    elif not first:
                        sp.wait_ge(slot_full, use(it, U_HEAD + 4 * (p + PM) + 4) - USES)
                    for c in range(4):
                        sp.dma_start(kop[32 * c:32 * c + 32, p % PM, :].bitcast(F32),
                                     (kh, kl, kh, kl)[c][r:r + 32, m, :].bitcast(F32)).then_inc(op_ready[p % PM], 16)
                        sp.dma_start(qop[32 * c:32 * c + 32, p % PM, :, :].bitcast(F32),
                                     (qh, ql, ql, qh)[c][r:r + 32, m, :, :].bitcast(F32)).then_inc(op_ready[p % PM], 16)
                    if p == PM - 1:
                        if not last:
                            sp.wait_ge(x_split, it * 2 + 2)
                            sp.dma_start(xT[:, :, :], xT_in[it + 1]).then_inc(xT_loaded, 16)
                        if not first:
                            store(it - 1)
                            sp.wait_ge(y_step, it * STEPS - (STEPS - 1))
                        sp.dma_start(xrow[:, :, :], x_in[it]).then_inc(xrow_loaded, 16)

            def store(it):
                sp.wait_ge(y_ready, it * NT + NT)
                sp.dma_start(ybuf[1:TOK + 1, :].rearrange("(b t p) d -> b p t d", p=P, t=NT)[it],
                             y[:, :, :]).then_inc(y_stored, 16)

            batches(sp, body)
            store(B - 1)
            sp.wait_ge(y_stored, 16 * B)
            sp.wait_ge(small_loaded, 64)

        @block.gpsimd
        def _(pool):
            pool.memset(zrow[:, :], 0.0).then_inc(zeroed, 1)
            pool.iota(part_i[:, :], [[0, 1]], base=0, channel_multiplier=1).then_inc(consts, 1)
            pool.memset(ident[:, :], 0.0).then_inc(masks, 1)
            pool.memset(mask[:, :, :], 1.0).then_inc(masks, 1)
            pool.memset(values[:, :, :, HD:2 * HD], 1.0).then_inc(consts, 1)
            pool.wait_ge(masks, 2)
            pool.affine_select(out=ident[:, :], in_=ident[:, :], compare_op=ALU.not_equal, fill=1.0, base=0,
                               pattern=[[-1, P]], channel_multiplier=1).then_inc(consts, 1)
            pool.affine_select(out=mask[:, :, :], in_=mask[:, :, :], compare_op=ALU.is_ge, fill=0.0, base=0,
                               pattern=[[0, 2], [1, P]], channel_multiplier=-1).then_inc(masks, 1)
            pool.wait_ge(masks, 3)

            def split_x(b):
                pool.wait_ge(xT_loaded, b * 16 + 16)
                pool.sem_inc(pool_passed, 1)
                if not (isinstance(b, int) and b == 0):
                    pool.wait_ge(slot_full, use(b, U_V + NT + 1) - USES if not (isinstance(b, int) and b == 1)
                                 else use(0, U_V + NT) + 1)
                    pool.sem_inc(pool_passed, 1)
                pool.tensor_copy(xh[:, :, :], xT[:, :, :]).then_inc(x_split, 1)
                pool.wait_ge(x_split, b * 2 + 1)
                pool.tensor_tensor(xl[:, :, :], xT[:, :, :], xh[:, :, :].bitcast(F32), ALU.subtract).then_inc(x_split, 1)

            split_x(0)

            def body(it, first, last):
                for h in range(H):
                    w = weights[:, h % 2, :]
                    pool.wait_ge(halved, it * (2 * H) + (2 * h + 1))
                    pool.tensor_tensor(w[:, 512:640], w[:, 512:640], mask[:, 0, :], ALU.mult).then_inc(masked, 1)
                    pool.wait_ge(halved, it * (2 * H) + (2 * h + 2))
                    pool.tensor_tensor(w[:, 1024:1152], w[:, 1024:1152], mask[:, 0, :], ALU.mult).then_inc(masked, 1)
                    late = w[:, 1408:1664].rearrange("p (a c) -> p a c", a=2)
                    pool.tensor_tensor(late, late, mask[:, :, :], ALU.mult).then_inc(masked, 1)
                    if h == 8 and not last:
                        split_x(it + 1)

            batches(pool, body)

        @block.scalar
        def _(act):
            def body(it, first, last):
                def square(h):
                    for half, (a, b) in enumerate(HALVES):
                        u = U_HEAD + 2 * h + half
                        act.wait_ge(slot_full, use(it, u) + 1)
                        if h >= 2 or not first:
                            act.wait_ge(o_full, it * H + (h - 1))
                        act.activation(weights[:, h % 2, a:b], slot[half][:, 0:b - a], ACT.Square,
                                       bias=HALF_ROOT).then_inc(squared, 1)

                def denominator(h):
                    src, dst = (HD, 0) if h % 2 == 0 else (0, HD)
                    act.wait_ge(o_full, it * H + (h + 1))
                    if h >= 4 or not first:
                        act.wait_ge(o_free, it * H + (h - 3))
                    act.activation(recip[dst:dst + HD, (h // 2) % 2, :], osum[h % 2][src:src + HD, :],
                                   ACT.Identity, bias=EPS_Z).then_inc(d_ready, 1)

                act.wait_ge(slot_full, use(it, U_Q) + 1)
                if first:
                    act.wait_ge(cq_ready, 4)
                for s in range(2):
                    act.activation(qh[:, :, s, :], slot[0][:, :].rearrange("p (m n) -> p m n", m=2), ACT.Copy,
                                   scale=cq[:, s:s + 1]).then_inc(qk_hi, 1)
                act.wait_ge(slot_full, use(it, U_K) + 1)
                act.activation(kh[:, :, 0:N], slot[1][:, :].rearrange("p (m n) -> p m n", m=2),
                               ACT.Copy).then_inc(qk_hi, 1)
                act.wait_ge(slot_full, use(it, U_KE) + 1)
                act.activation(kh[:, :, N:NK], slot[0][:, 0:2 * P].rearrange("p (m n) -> p m n", m=2),
                               ACT.Copy).then_inc(qk_hi, 1)
                if not first:
                    deviation(it - 1)
                for h in range(H):
                    square(h)
                    if h >= 1:
                        denominator(h - 1)
                denominator(H - 1)

            def deviation(b):
                act.wait_ge(y_step, b * STEPS + (STEPS - 1))
                act.activation(sdev[:, :], mv[:, :, 1], ACT.Sqrt, bias=EPS_LN).then_inc(sd_ready, 1)

            batches(act, body)
            deviation(B - 1)

        @block.vector
        def _(dve):
            dve.wait_ge(consts, 1)
            dve.tensor_scalar(odd_i[:, :], part_i[:, :], 4, 1, ALU.logical_shift_right,
                              ALU.bitwise_and).then_inc(cq_ready, 1)
            dve.wait_ge(cq_ready, 1)
            dve.tensor_copy(cq[:, 0:1], odd_i[:, :]).then_inc(cq_ready, 1)
            dve.wait_ge(cq_ready, 2)
            dve.tensor_scalar(cq[:, 1:2], cq[:, 0:1], CQ, None, ALU.mult).then_inc(cq_ready, 1)
            dve.wait_ge(cq_ready, 3)
            dve.tensor_scalar(cq[:, 0:1], cq[:, 1:2], -1.0, CQ, ALU.mult, ALU.add).then_inc(cq_ready, 1)
            for n, (kind, c) in enumerate(CHUNKS):
                hi, lo = (wqk_h, wqk_l) if kind == 0 else (wv_h, wv_l)
                if kind == 0:
                    hi, lo = hi[:, c, :, :].rearrange("p k n -> p (k n)"), lo[:, c, :, :].rearrange("p k n -> p (k n)")
                else:
                    hi, lo = hi[:, c // 2, c % 2, :], lo[:, c // 2, c % 2, :]
                raw = weights[:, n % 2, 0:hi.shape[1]]
                dve.wait_ge(w_loaded[n % 2], 16 * (n // 2 + 1))
                dve.tensor_copy(hi, raw).then_inc(w_split, 1)
                dve.wait_ge(w_split, 2 * n + 1)
                dve.tensor_tensor(lo, raw, hi.bitcast(F32), ALU.subtract).then_inc(w_split, 1)
            dve.wait_ge(cq_ready, 4)

            def body(it, first, last):
                def low(dst, src, factor, hi, ready, free):
                    dve.wait_ge(qk_hi, it * 4 + max(ready, 2))
                    op = dve.scalar_tensor_tensor(dst, src, factor, hi.bitcast(F32), ALU.mult, ALU.subtract)
                    op.then_inc(qk_lo, 1)
                    if free is not None:
                        dve.wait_ge(qk_lo, it * 4 + ready)
                        dve.sem_inc(slot_free[free], 1)

                def store_values(t):
                    u = U_V + t
                    dve.wait_ge(slot_full, use(it, u) + 1)
                    if t == 0 and not first:
                        dve.wait_ge(o_full, it * H)
                    dst = values[:, t, :, :].rearrange("p a (s d) -> p a s d", s=3)[:, :, 0:3:2, :]
                    dve.tensor_copy(dst, slot[u % 2][:, :].rearrange("p (a s d) -> p a s d", s=2, d=HD))\
                       .then_inc(slot_free[u % 2], 1)

                def half(h):
                    for k, (a, b) in enumerate(HALVES):
                        dve.wait_ge(squared, it * (2 * H) + (2 * h + k + 1))
                        dve.tensor_scalar(weights[:, h % 2, a:b], weights[:, h % 2, a:b], 0.5, None,
                                          ALU.add).then_inc(halved, 1)

                def divide(h):
                    s = HD * (h % 2)
                    r = recip[s:s + HD, (h // 2) % 2, :]
                    dve.wait_ge(d_ready, it * H + (h + 1))
                    dve.reciprocal(r, r).then_inc(r_ready, 1)
                    dve.wait_ge(r_ready, it * H + (h + 1))
                    if h >= 4 or not first:
                        dve.wait_ge(att_used, it * PAIRS + (h // 2 - 1))
                    dve.tensor_tensor(att[s:s + HD, (h // 2) % 2, :], osum[h % 2][s:s + HD, :], r,
                                      ALU.mult).then_inc(o_free, 1)

                m2 = "p (m n) -> p m n"
                for s in range(2):
                    low(ql[:, :, s, :], slot[0][:, :].rearrange(m2, m=2), cq[:, s:s + 1], qh[:, :, s, :],
                        1 + s, 0 if s else None)
                low(kl[:, :, 0:N], slot[1][:, :].rearrange(m2, m=2), 1.0, kh[:, :, 0:N], 3, 1)
                low(kl[:, :, N:NK], slot[0][:, 0:2 * P].rearrange(m2, m=2), 1.0, kh[:, :, N:NK], 4, 0)
                store_values(0)
                store_values(1)
                if not first:
                    moments(it - 1)
                store_values(2)
                if not first:
                    normalise(it - 1)
                store_values(3)
                store_values(4)
                if not first:
                    logits_of(it, it - 1)
                for h in range(H):
                    half(h)
                    if h >= 1:
                        divide(h - 1)
                divide(H - 1)

            def moments(b):
                dve.wait_ge(att_used, b * PAIRS + PAIRS)
                dve.wait_ge(xrow_loaded, b * 16 + 16)
                if not (isinstance(b, int) and b == 0):
                    dve.wait_ge(y_stored, b * 16)
                dve.tensor_tensor(y[:, :, :], ysum[:, :].rearrange("p (t d) -> p t d", t=NT), xrow[:, :, :],
                                  ALU.add).then_inc(y_step, 1)
                dve.wait_ge(y_step, b * STEPS + 1)
                for t in range(NT):
                    dve.bn_stats(stats[:, t, :], y[:, t, :]).then_inc(y_step, 1)
                dve.wait_ge(y_step, b * STEPS + (1 + NT))
                dve.sem_inc(dve_passed, 1)
                for t in range(NT):
                    dve.bn_aggr(mv[:, t, :], stats[:, t, :]).then_inc(y_step, 1)

            def normalise(b):
                dve.wait_ge(sd_ready, b + 1)
                dve.reciprocal(rstd[:, :], sdev[:, :]).then_inc(y_step, 1)
                dve.wait_ge(y_step, b * STEPS + STEPS)
                for t in range(NT):
                    dve.tensor_scalar(y[:, t, :], y[:, t, :], mv[:, t, 0:1], rstd[:, t:t + 1], ALU.subtract,
                                      ALU.mult).then_inc(y_ready, 1)

            def logits_of(it, b):
                dve.wait_ge(slot_full, use(it, U_YT) + 1)
                dve.tensor_copy(yT[:, :, :], slot[0][:, :].rearrange("p (t n) -> p t n", n=P)).then_inc(yT_ready, 1)
                dve.wait_ge(yT_ready, b + 1)
                dve.sem_inc(slot_free[0], 1)
                dve.wait_ge(slot_full, use(it, U_LG) + 1)
                dve.tensor_tensor(logits[:, bass.ts(b, NT), :], slot[1][:, 0:NT * E].rearrange("p (t e) -> p t e", e=E),
                                  br[:, :].unsqueeze(1).to_broadcast([P, NT, E]), ALU.add).then_inc(slot_free[1], 1)

            batches(dve, body)
            moments(B - 1)
            normalise(B - 1)
            logits_of(B, B - 1)

        @block.tensor
        def _(pe):
            def three(dst, wh, wl, vh, vl):
                parts = [(wh, vh), (wh, vl), (wl, vh)]
                for n, (a, b) in enumerate((a, b) for a in range(3) for b in range(KD)):
                    last = pe.matmul(dst, parts[a][0](b), parts[a][1](b), start=(n == 0), stop=(n == 3 * KD - 1))
                return last

            def take(it, u):
                if isinstance(it, int) and it == 0:
                    if u >= 2:
                        pe.wait_ge(slot_free[u % 2], u // 2)
                elif u < 2 or (isinstance(it, int) and it == B):
                    pe.wait_ge(squared, it * (2 * H))
                else:
                    pe.wait_ge(slot_free[u % 2], it * FREED + (u // 2 - 1))

            def transposed_rows(it, b):
                pe.wait_ge(y_ready, b * NT + NT)
                take(it, U_YT)
                for t in range(NT):
                    for k in range(KD):
                        n = t * KD + k
                        last = pe.transpose(slot[0][:, n * P:(n + 1) * P], y[:, t, k * P:(k + 1) * P], ident[:, :])
                last.then_inc(slot_full, 1)

            def router(it, b):
                take(it, U_LG)
                pe.wait_ge(yT_ready, b + 1)
                for t in range(NT):
                    for k in range(KD):
                        last = pe.matmul(slot[1][:, t * E:(t + 1) * E], yT[:, t * KD + k, :], wr[:, k, :],
                                         start=(k == 0), stop=(k == KD - 1))
                last.then_inc(slot_full, 1)

            def output(it, p):
                pe.wait_ge(o_free, it * H + (2 * p + 2))
                if p == 0 and not (isinstance(it, int) and it == 0):
                    pe.wait_ge(y_step, it * STEPS - (STEPS - 1))
                for t in range(NT):
                    last = pe.matmul(ysum[:, t * D:(t + 1) * D], att[:, p % 2, t * P:(t + 1) * P], wo[:, p, :],
                                     start=(p == 0 and t % 2 == 0), stop=(p == PAIRS - 1), skip_group_check=True)
                    if t == NT - 1:
                        last.then_inc(att_used, 1)

            def body(it, first, last_batch):
                def project_qk(u, w, cols, sl):
                    take(it, u)
                    for m in range(2):
                        lo, hi = m * P, (m + 1) * P
                        last = three(slot[sl][:, m * cols:(m + 1) * cols],
                                     lambda k: wqk_h[:, w, k, lo:hi], lambda k: wqk_l[:, w, k, lo:hi],
                                     lambda k: xh[:, k, 0:cols], lambda k: xl[:, k, 0:cols])
                    last.then_inc(slot_full, 1)

                def project_values(t):
                    u, enc = U_V + t, int(t == NT)
                    a = 0 if enc else t * P
                    take(it, u)
                    for c in range(2):
                        last = three(slot[u % 2][:, c * 512:(c + 1) * 512],
                                     lambda k: xh[:, k, a:a + P], lambda k: xl[:, k, a:a + P],
                                     lambda k: wv_h[:, enc, k, c * 512:(c + 1) * 512],
                                     lambda k: wv_l[:, enc, k, c * 512:(c + 1) * 512])
                    last.then_inc(slot_full, 1)

                def scores(h, half):
                    p = h // 2
                    if h % 2 == 0 and half == 0:
                        pe.wait_ge(op_ready[p % PM], it * 256 + (128 if p < PM else 256))
                    if h == 0:
                        pe.wait_ge(slot_free[half], it * FREED + (FREED - 1))
                    else:
                        pe.wait_ge(squared, it * (2 * H) + (2 * h + half - 1))
                    off = HALVES[half][0]
                    for j, q0, col in BLOCKS[2 * half:2 * half + 2 + half]:
                        k0 = j * P
                        last = pe.matmul(slot[half][:, col - off:col - off + N - q0], kop[:, p % PM, k0:k0 + P],
                                         qop[:, p % PM, h % 2, q0:N], start=True, stop=True)
                    last.then_inc(slot_full, 1)

                def weigh(h, half):
                    s = HD * (h % 2)
                    if half == 0:
                        pe.wait_ge(masked, it * (3 * H) + (3 * h + 1))
                        if h >= 2 or not first:
                            pe.wait_ge(o_free, it * H + (h - 1))
                    else:
                        pe.wait_ge(masked, it * (3 * H) + (3 * h + 3))
                    for n, (j, q0, col) in enumerate(BLOCKS[2 * half:2 * half + 2 + half]):
                        done = half == 1 and n == 2
                        last = pe.matmul(osum[h % 2][:, q0:N], values[:, j, h // 2, s:s + 2 * HD],
                                         weights[:, h % 2, col:col + N - q0], start=(half == 0 and n == 0), stop=done)
                    if half == 1:
                        last.then_inc(o_full, 1)

                if first:
                    pe.wait_ge(w_split, 6)
                pe.wait_ge(x_split, it * 2 + 2)
                project_qk(U_Q, 0, N, 0)
                project_qk(U_K, 1, N, 1)
                project_qk(U_KE, 2, P, 0)
                if first:
                    pe.wait_ge(w_split, 2 * len(CHUNKS))
                    pe.wait_ge(small_loaded, 64)
                    pe.wait_ge(consts, 3)
                else:
                    last_output(it - 1)
                for t in range(NT + 1):
                    project_values(t)
                if not first:
                    transposed_rows(it, it - 1)
                    router(it, it - 1)
                scores(0, 0)
                scores(0, 1)
                for h in range(H):
                    if h + 1 < H:
                        scores(h + 1, 0)
                    weigh(h, 0)
                    if h + 1 < H:
                        scores(h + 1, 1)
                    weigh(h, 1)
                    if h >= 2 and h % 2 == 0:
                        output(it, h // 2 - 1)

            def last_output(b):
                output(b, PAIRS - 1)

            batches(pe, body)
            last_output(B - 1)
            transposed_rows(B, B - 1)
            router(B, B - 1)


def experts(nc, sem, w1_in, b1_in, w2_in, b2_in, ybuf, logits, ident, out):
    with ExitStack() as ctx:
        def sb(name, shape, dt=F32):
            return ctx.enter_context(nc.sbuf_tensor(name, shape, dt))

        def ps(name, shape):
            return ctx.enter_context(nc.psum_tensor(name, shape, F32))

        w1 = sb("w1", [P, E, KD, I])
        w2 = sb("w2", [P, E, IC, D])
        b1 = sb("b1", [P, E * IC])
        b2 = sb("b2", [P, E * D])
        row_index = sb("row_index", [P, SLOTS], I32)
        out_index = sb("out_index", [P, SLOTS], I32)
        gates = sb("gates", [P, SLOTS])
        expert_of = sb("expert_of", [P, SLOTS], I32)

        w_seq = sem("expert_weights")
        table_loaded = sem("table_loaded")
        w_sem = [sem("expert_loaded0"), sem("expert_loaded1")]
        routed = sem("routed")

        with ExitStack() as inner:
            route(nc, inner, sem, w_seq, table_loaded, w_sem, routed, w1, w2, b1, b2, w1_in, w2_in, b1_in, b2_in,
                  logits, row_index, out_index, gates, expert_of)
        run_experts(nc, ctx, sem, w_seq, w1, w2, b1, b2, row_index, out_index, gates, expert_of,
                    ybuf, ident, out, w_sem, w1_in, w2_in)


LOADED_EARLY = 2


def load_expert(sp, e, w1, w2, w1_in, w2_in, w_sem):
    sp.dma_start(w1[:, e, :, :], w1_in[:, e, :, :]).then_inc(w_sem[e % 2], 16)
    sp.dma_start(w2[:, e, :, :], w2_in[:, e, :, :]).then_inc(w_sem[e % 2], 16)


def route(nc, ctx, sem, w_seq, table_loaded, w_sem, routed, w1, w2, b1, b2, w1_in, w2_in, b1_in, b2_in,
          logits, row_index, out_index, gates, expert_of):
    def sb(name, shape, dt=F32):
        return ctx.enter_context(nc.sbuf_tensor(name, shape, dt))

    def ps(name, shape):
        return ctx.enter_context(nc.psum_tensor(name, shape, F32))

    falling = sb("falling", [P, E])
    tile_starts = sb("tile_starts", [P, TT])
    count128 = sb("count128", [P, P])
    token1 = sb("token1", [P, TT])
    before = sb("before", [P, P], BF16)
    ones = sb("ones", [P, P], BF16)
    ones32 = sb("ones32", [P, TT])
    top = sb("top", [P, TT])
    second = sb("second", [P, TT])
    key = sb("key", [P, TT, E])
    hot = sb("hot", [P, TT, E])
    hotb = sb("hotb", [P, TT, E], BF16)
    rest = sb("rest", [P, TT, E])
    gate = sb("gate", [P, TT])
    kmax = sb("kmax", [P, TT])
    cum = sb("cum", [P, E, TT])
    more = sb("more", [P, E, TT])
    used = sb("used", [P, E])
    last_slot = sb("last_slot", [P, E])
    first_row = sb("first_row", [P, E])
    place = sb("place", [P, TT, E])
    pos = sb("pos", [P, TT])
    pos_i = sb("pos_i", [P, TT], I32)
    slot_i = sb("slot_i", [P, TT], I32)
    row_i = sb("row_i", [P, TT], I32)
    slot_f = sb("slot_f", [P, TT])
    row_f = sb("row_f", [P, TT])
    in_slot = sb("in_slot", [P, TT, SLOTS])
    carried = sb("carried", [P, TT, 2, SLOTS])
    in_row = sb("in_row", [P, TT, P])
    passed = sb("passed", [P, SLOTS, E - 1])
    expert_f = sb("expert_f", [P, SLOTS])
    index_f = sb("index_f", [P, SLOTS])
    empty = sb("empty", [P, SLOTS])
    ranks = ps("ranks", [P, TT * E])
    totals = ps("totals", [P, TT * E])
    found = ps("found", [P, 2 * SLOTS])

    made = sem("route_consts")
    step = sem("route_step")
    counted = sem("counted")
    exp_in, exp_out = sem("exp_in"), sem("exp_out")
    placed = sem("placed")
    found_all = sem("found_all")

    block = ctx.enter_context(nc.Block())

    @block.sync
    def _(sp):
        sp.dma_start(b1[:, :], b1_in).then_inc(table_loaded, 16)
        sp.dma_start(b2[:, :], b2_in.partition_broadcast(P)).then_inc(table_loaded, 16)
        for e in range(LOADED_EARLY):
            load_expert(sp, e, w1, w2, w1_in, w2_in, w_sem)
        sp.wait_ge(table_loaded, 32)

    @block.gpsimd
    def _(pool):
        pool.iota(falling[:, :], [[-1, E]], base=E, channel_multiplier=0,
                  allow_small_or_imprecise_dtypes=True).then_inc(made, 1)
        pool.iota(tile_starts[:, :], [[P, TT]], base=0, channel_multiplier=0,
                  allow_small_or_imprecise_dtypes=True).then_inc(made, 1)
        pool.iota(count128[:, :], [[1, P]], base=0, channel_multiplier=0,
                  allow_small_or_imprecise_dtypes=True).then_inc(made, 1)
        pool.iota(token1[:, :], [[P, TT]], base=1, channel_multiplier=1,
                  allow_small_or_imprecise_dtypes=True).then_inc(made, 1)
        pool.memset(ones32[:, :], 1.0).then_inc(made, 1)
        pool.memset(ones[:, :], 1.0).then_inc(made, 1)
        pool.memset(before[:, :], 1.0).then_inc(made, 1)
        pool.wait_ge(made, 7)
        pool.affine_select(out=before[:, :], in_=before[:, :], compare_op=ALU.is_gt, fill=0.0, base=0,
                           pattern=[[1, P]], channel_multiplier=-1).then_inc(made, 1)

    @block.scalar
    def _(act):
        act.wait_ge(exp_in, 1)
        act.activation(gate[:, :], second[:, :], ACT.Exp).then_inc(exp_out, 1)

    @block.tensor
    def _(pe):
        pe.wait_ge(made, 8)
        pe.wait_ge(counted, 1)
        flat = hotb[:, :, :].rearrange("p t e -> p (t e)")
        pe.matmul(ranks[:, :], before[:, :], flat, start=True, stop=True)
        pe.matmul(totals[:, :], ones[:, :], flat, start=True, stop=True).then_inc(counted, 1)
        pe.wait_ge(placed, 1)
        for t in range(TT):
            last = pe.matmul(found[:, :], in_row[:, t, :], carried[:, t, :, :].rearrange("p a s -> p (a s)"),
                             start=(t == 0), stop=(t == TT - 1))
        last.then_inc(found_all, 1)

    @block.vector
    def _(dve):
        n = [0]

        def after(op):
            n[0] += 1
            op.then_inc(step, 1)
            dve.wait_ge(step, n[0])

        def over_e(ap):
            return ap.unsqueeze(2).to_broadcast([P, TT, E])

        def over_t(ap):
            return ap.unsqueeze(1).to_broadcast([P, TT, E])

        dve.wait_ge(made, 8)
        after(dve.tensor_reduce(top[:, :], logits[:, :, :], AX.X, ALU.max))
        after(dve.tensor_tensor(key[:, :, :], logits[:, :, :], over_e(top[:, :]), ALU.is_ge))
        after(dve.tensor_tensor(key[:, :, :], key[:, :, :], over_t(falling[:, :]), ALU.mult))
        after(dve.tensor_reduce(kmax[:, :], key[:, :, :], AX.X, ALU.max))
        after(dve.tensor_tensor(hot[:, :, :], over_t(falling[:, :]), over_e(kmax[:, :]), ALU.is_equal))
        after(dve.tensor_copy(hotb[:, :, :], hot[:, :, :]))
        dve.sem_inc(counted, 1)
        after(dve.scalar_tensor_tensor(rest[:, :, :], hot[:, :, :], -3.0e38, logits[:, :, :], ALU.mult, ALU.add))
        after(dve.tensor_reduce(second[:, :], rest[:, :, :], AX.X, ALU.max))
        after(dve.tensor_tensor(second[:, :], second[:, :], top[:, :], ALU.subtract))
        dve.sem_inc(exp_in, 1)
        dve.wait_ge(counted, 2)
        by_tile = totals[:, :].rearrange("p (t e) -> p t e", e=E)
        for e in range(E):
            op = dve.tensor_tensor_scan(cum[:, e, :], ones32[:, :], by_tile[:, :, e], 0.0, ALU.mult, ALU.add)
            if e < E - 1:
                n[0] += 1
                op.then_inc(step, 1)
        after(op)
        after(dve.tensor_tensor(more[:, :, :], cum[:, :, TT - 1:TT].to_broadcast([P, E, TT]),
                                tile_starts[:, :].unsqueeze(1).to_broadcast([P, E, TT]), ALU.is_gt))
        after(dve.tensor_reduce(used[:, :], more[:, :, :], AX.X, ALU.add))
        after(dve.tensor_scalar(used[:, :], used[:, :], 1.0, None, ALU.max))
        after(dve.tensor_tensor_scan(last_slot[:, :], ones32[:, 0:E], used[:, :], 0.0, ALU.mult, ALU.add))
        after(dve.tensor_tensor(first_row[:, :], last_slot[:, :], used[:, :], ALU.subtract))
        after(dve.tensor_scalar(first_row[:, :], first_row[:, :], float(P), None, ALU.mult))
        after(dve.tensor_tensor(place[:, :, :], cum[:, :, :].rearrange("p e t -> p t e"), by_tile, ALU.subtract))
        after(dve.tensor_tensor(place[:, :, :], place[:, :, :], ranks[:, :].rearrange("p (t e) -> p t e", e=E),
                                ALU.add))
        after(dve.tensor_tensor(place[:, :, :], place[:, :, :], over_t(first_row[:, :]), ALU.add))
        after(dve.tensor_tensor(place[:, :, :], place[:, :, :], hot[:, :, :], ALU.mult))
        after(dve.tensor_reduce(pos[:, :], place[:, :, :], AX.X, ALU.add))
        after(dve.tensor_copy(pos_i[:, :], pos[:, :]))
        after(dve.tensor_scalar(slot_i[:, :], pos_i[:, :], 7, None, ALU.logical_shift_right))
        after(dve.tensor_scalar(row_i[:, :], pos_i[:, :], P - 1, None, ALU.bitwise_and))
        after(dve.tensor_copy(slot_f[:, :], slot_i[:, :]))
        after(dve.tensor_copy(row_f[:, :], row_i[:, :]))
        after(dve.tensor_tensor(in_row[:, :, :], count128[:, :].unsqueeze(1).to_broadcast([P, TT, P]),
                                row_f[:, :].unsqueeze(2).to_broadcast([P, TT, P]), ALU.is_equal))
        after(dve.tensor_tensor(in_slot[:, :, :], count128[:, 0:SLOTS].unsqueeze(1).to_broadcast([P, TT, SLOTS]),
                                slot_f[:, :].unsqueeze(2).to_broadcast([P, TT, SLOTS]), ALU.is_equal))
        dve.wait_ge(exp_out, 1)
        after(dve.tensor_scalar(gate[:, :], gate[:, :], 1.0, None, ALU.add))
        after(dve.reciprocal(gate[:, :], gate[:, :]))
        after(dve.tensor_tensor(carried[:, :, 0, :], in_slot[:, :, :],
                                token1[:, :].unsqueeze(2).to_broadcast([P, TT, SLOTS]), ALU.mult))
        after(dve.tensor_tensor(carried[:, :, 1, :], in_slot[:, :, :],
                                gate[:, :].unsqueeze(2).to_broadcast([P, TT, SLOTS]), ALU.mult))
        dve.sem_inc(placed, 1)
        after(dve.tensor_tensor(passed[:, :, :], count128[:, 0:SLOTS].unsqueeze(2).to_broadcast([P, SLOTS, E - 1]),
                                last_slot[:, 0:E - 1].unsqueeze(1).to_broadcast([P, SLOTS, E - 1]), ALU.is_ge))
        after(dve.tensor_reduce(expert_f[:, :], passed[:, :, :], AX.X, ALU.add))
        after(dve.tensor_copy(expert_of[:, :], expert_f[:, :]))
        dve.wait_ge(found_all, 1)
        after(dve.tensor_copy(row_index[:, :], found[:, 0:SLOTS]))
        after(dve.tensor_copy(gates[:, :], found[:, SLOTS:2 * SLOTS]))
        after(dve.tensor_scalar(empty[:, :], found[:, 0:SLOTS], 0.0, float(SKIP + 1), ALU.is_equal, ALU.mult))
        after(dve.scalar_tensor_tensor(index_f[:, :], found[:, 0:SLOTS], -1.0, empty[:, :], ALU.add, ALU.add))
        after(dve.tensor_copy(out_index[:, :], index_f[:, :]))
        dve.sem_inc(routed, 1)


def run_experts(nc, ctx, sem, w_seq, w1, w2, b1, b2, row_index, out_index, gates, expert_of,
                ybuf, ident, out, w_sem, w1_in, w2_in):
    RING = 4
    UNROLL = 4
    PEELED = 3

    def sb(name, shape, dt=F32):
        return ctx.enter_context(nc.sbuf_tensor(name, shape, dt))

    def ps(name, shape):
        return ctx.enter_context(nc.psum_tensor(name, shape, F32))

    rows = sb("rows", [P, RING, D])
    rows_col = sb("rows_col", [P, RING], I32)
    out_col = sb("out_col", [P, 2], I32)
    rowsT = sb("rowsT", [P, 2, KD, P])
    inner = sb("inner", [P, 2, I])
    active = sb("active", [P, 2, IC, P])
    result = sb("result", [P, 2, D])
    centred = sb("centred", [P, 2, D])
    final = sb("final", [P, 2, D])
    stats = sb("e_stats", [P, 2, 6])
    mv = sb("e_mv", [P, 2, 2])
    rs = sb("e_rs", [P, 2])
    eps = sb("eps", [P, 1])
    minus_half = sb("minus_half", [P, 1])

    turned = ps("turned", [P, KD * P])
    up = ps("up", [P, I])
    upT = ps("upT", [P, I])
    down = [ps("down0", [P, D]), ps("down1", [P, D])]

    gathered = [sem(f"gathered{i}") for i in range(RING)]
    indexed, ready_consts = sem("indexed"), sem("loop_consts")
    turned_full, rowsT_ready = sem("turned_full"), sem("rowsT_ready")
    up_full, inner_ready = sem("up_full"), sem("inner_ready")
    upT_full, active_ready = sem("upT_full"), sem("active_ready")
    down_full, down_read = sem("down_full"), sem("down_read")
    norm_step, final_step = sem("norm_step"), sem("final_step")
    scattered = [sem("scattered0"), sem("scattered1")]
    passed, dve_passed = sem("loop_passed"), sem("loop_dve_passed")
    NORM = 4
    FINAL = 4

    def steps(eng, body):
        for s in range(PEELED):
            body(s, s)
        loops = (SLOTS - PEELED - 1) // UNROLL
        with eng.Fori(0, loops) as i:
            for j in range(UNROLL):
                body(i * UNROLL + (PEELED + j), PEELED + j)
        for s in range(PEELED + loops * UNROLL, SLOTS):
            body(s, s)

    def expert(eng, s):
        return eng.value_load(expert_of[0:1, bass.ds(s, 1)], min_val=0, max_val=E - 1)

    block = ctx.enter_context(nc.Block())

    @block.sync
    def _(sp):
        for e in range(LOADED_EARLY, E):
            load_expert(sp, e, w1, w2, w1_in, w2_in, w_sem)
            sp.wait_ge(w_sem[(e - 1) % 2], 32 * ((e - 1) // 2 + 1))
            if e - 1 == LOADED_EARLY - 1:
                sp.sem_inc(w_seq, LOADED_EARLY)
            else:
                sp.sem_inc(w_seq, 1)
        sp.wait_ge(w_sem[(E - 1) % 2], 32 * ((E - 1) // 2 + 1))
        sp.sem_inc(w_seq, 1)

    @block.gpsimd
    def _(pool):
        pool.memset(eps[:, :], EPS_LN).then_inc(ready_consts, 1)
        pool.memset(minus_half[:, :], -0.5).then_inc(ready_consts, 1)
        pool.wait_ge(ready_consts, 2)

        def gather(s, k):
            pool.tensor_copy(rows_col[:, k % RING:k % RING + 1], row_index[:, bass.ds(s, 1)]).then_inc(indexed, 1)
            pool.wait_ge(indexed, s + 1)
            pool.sem_inc(passed, 1)
            pool.indirect_dma_start(rows[:, k % RING, :], None, ybuf[:, :],
                                    bass.IndirectOffsetOnAxis(ap=rows_col[:, k % RING:k % RING + 1], axis=0))\
                .then_inc(gathered[k % RING], 16)

        def finish(s, k):
            p = k % 2
            if not (isinstance(s, int) and s < 2):
                pool.wait_ge(scattered[p], (s - p) * 8)
                pool.sem_inc(passed, 1)
            pool.tensor_copy(out_col[:, p:p + 1], out_index[:, bass.ds(s, 1)]).then_inc(final_step, 1)
            pool.wait_ge(norm_step, s * NORM + NORM)
            pool.tensor_tensor(rs[:, p:p + 1], mv[:, p, 1:2], eps[:, :], ALU.add).then_inc(final_step, 1)
            pool.wait_ge(final_step, s * FINAL + 2)
            pool.tensor_tensor(rs[:, p:p + 1], rs[:, p:p + 1], minus_half[:, :], ALU.pow).then_inc(final_step, 1)
            pool.wait_ge(final_step, s * FINAL + 3)
            pool.tensor_tensor(final[:, p, :], centred[:, p, :], rs[:, p:p + 1].to_broadcast([P, D]),
                               ALU.mult).then_inc(final_step, 1)
            pool.wait_ge(final_step, s * FINAL + 4)
            pool.sem_inc(passed, 1)
            pool.indirect_dma_start(out, bass.IndirectOffsetOnAxis(ap=out_col[:, p:p + 1], axis=0), final[:, p, :],
                                    None, bounds_check=TOK - 1, oob_is_err=False).then_inc(scattered[p], 16)

        for s in range(3):
            gather(s, s)
        finish(0, 0)
        gather(3, 3)
        with pool.Fori(0, (SLOTS - 7) // UNROLL) as i:
            for j in range(UNROLL):
                gather(i * UNROLL + (4 + j), 4 + j)
                finish(i * UNROLL + (1 + j), 1 + j)
        for s in range(SLOTS - 6, SLOTS):
            if s + 3 < SLOTS:
                gather(s + 3, s + 3)
            finish(s, s)
        for p in range(2):
            pool.wait_ge(scattered[p], 16 * ((SLOTS + 1 - p) // 2))

    @block.scalar
    def _(act):
        def turn(s, k):
            act.wait_ge(turned_full, s + 1)
            if not (isinstance(s, int) and s < 2):
                act.wait_ge(up_full, s - 1)
            act.activation(rowsT[:, k % 2, :, :], turned[:, :].rearrange("p (k n) -> p k n", k=KD),
                           ACT.Copy).then_inc(rowsT_ready, 1)

        def body(s, k):
            if not (isinstance(s, int) and s == SLOTS - 1):
                turn(s + 1, k + 1)
            e = expert(act, s)
            act.wait_ge(upT_full, s + 1)
            if not (isinstance(s, int) and s < 2):
                act.wait_ge(down_full, s - 1)
            for c in range(IC):
                act.activation(active[:, k % 2, c, :], upT[:, c * P:(c + 1) * P], ACT.Gelu,
                               bias=b1[:, bass.ds(e * IC + c, 1)]).then_inc(active_ready, 1)

        turn(0, 0)
        steps(act, body)

    @block.vector
    def _(dve):
        def residual(s, k):
            p = k % 2
            e = expert(dve, s)
            dve.wait_ge(down_full, s + 1)
            if not (isinstance(s, int) and s < 2):
                dve.wait_ge(final_step, s * FINAL - FINAL)
            dve.tensor_tensor(result[:, p, :], down[p][:, :], b2[:, bass.ds(e * D, D)], ALU.add).then_inc(down_read, 1)
            dve.wait_ge(down_read, s + 1)
            dve.scalar_tensor_tensor(result[:, p, :], result[:, p, :], gates[:, bass.ds(s, 1)], rows[:, k % RING, :],
                                     ALU.mult, ALU.add).then_inc(norm_step, 1)
            dve.wait_ge(norm_step, s * NORM + 1)
            dve.bn_stats(stats[:, p, :], result[:, p, :]).then_inc(norm_step, 1)
            dve.wait_ge(norm_step, s * NORM + 2)
            dve.sem_inc(dve_passed, 1)
            dve.bn_aggr(mv[:, p, :], stats[:, p, :]).then_inc(norm_step, 1)
            dve.wait_ge(norm_step, s * NORM + 3)
            dve.tensor_scalar(centred[:, p, :], result[:, p, :], mv[:, p, 0:1], None,
                              ALU.subtract).then_inc(norm_step, 1)

        def body(s, k):
            dve.wait_ge(up_full, s + 1)
            if not (isinstance(s, int) and s < 2):
                dve.wait_ge(upT_full, s - 1)
            dve.tensor_copy(inner[:, k % 2, :], up[:, :]).then_inc(inner_ready, 1)
            if not (isinstance(s, int) and s == 0):
                residual(s - 1, k - 1)

        steps(dve, body)
        residual(SLOTS - 1, SLOTS - 1)

    @block.tensor
    def _(pe):
        def turn(s, k):
            pe.wait_ge(gathered[k % RING], (s - k % RING) * (16 // RING) + 16)
            if not (isinstance(s, int) and s == 0):
                pe.wait_ge(rowsT_ready, s)
            for c in range(KD):
                last = pe.transpose(turned[:, c * P:(c + 1) * P], rows[:, k % RING, c * P:(c + 1) * P], ident[:, :])
            last.then_inc(turned_full, 1)

        def second(s, k):
            e = expert(pe, s)
            pe.wait_ge(active_ready, s * IC + IC)
            if not (isinstance(s, int) and s < 2):
                pe.wait_ge(down_read, s - 1)
            for c in range(IC):
                last = pe.matmul(down[k % 2][:, :], active[:, k % 2, c, :], w2[:, bass.ds(e, 1), c, :].rearrange(
                    "p o d -> p (o d)"), start=(c == 0), stop=(c == IC - 1))
            last.then_inc(down_full, 1)

        def body(s, k):
            e = expert(pe, s)
            pe.wait_ge(w_seq, e + 1)
            pe.wait_ge(rowsT_ready, s + 1)
            if not (isinstance(s, int) and s == 0):
                pe.wait_ge(inner_ready, s)
            for h in range(I // 512):
                for c in range(KD):
                    last = pe.matmul(up[:, h * 512:(h + 1) * 512], rowsT[:, k % 2, c, :],
                                     w1[:, bass.ds(e, 1), c, h * 512:(h + 1) * 512].rearrange("p o d -> p (o d)"),
                                     start=(c == 0), stop=(c == KD - 1))
            last.then_inc(up_full, 1)
            if not (isinstance(s, int) and s == SLOTS - 1):
                turn(s + 1, k + 1)
            if not (isinstance(s, int) and s == 0):
                second(s - 1, k - 1)
            pe.wait_ge(inner_ready, s + 1)
            if not (isinstance(s, int) and s == 0):
                pe.wait_ge(active_ready, s * IC)
            for c in range(IC):
                last = pe.transpose(upT[:, c * P:(c + 1) * P], inner[:, k % 2, c * P:(c + 1) * P], ident[:, :])
            last.then_inc(upT_full, 1)

        turn(0, 0)
        steps(pe, body)
        second(SLOTS - 1, SLOTS - 1)


_OUT = (B, N, D)


def kernel(**inputs):
    import numpy as _np
    import concourse.bacc as _bacc
    from concourse.bass_utils import run_bass_kernel_spmd as _run

    a = {k: _np.asarray(v) for k, v in inputs.items()}
    x = a["L0_attn_x"]

    def by_row(w):
        return w.T.reshape(KD, P, w.shape[0]).transpose(1, 0, 2)

    wqk = _np.stack([by_row(a[n]) for n in ("L0_attn_Wq", "L0_attn_Wk", "L0_attn_Wk_enc")], 1).reshape(P, 3, KD * D)
    wv = _np.stack([by_row(a[n]) for n in ("L0_attn_Wv", "L0_attn_Wv_enc")], 1).reshape(P, 2 * KD, I)
    arrays = {
        "xT": x.transpose(0, 2, 1).reshape(B, KD, P, N).transpose(0, 2, 1, 3),
        "x": x.reshape(B, NT, P, D).transpose(0, 2, 1, 3),
        "wqk": wqk,
        "wv": wv,
        "wo": a["L0_attn_Wout"].T.reshape(PAIRS, P, D).transpose(1, 0, 2),
        "w1": a["L0_ffn_w1"].reshape(E, KD, P, I).transpose(2, 0, 1, 3),
        "b1": a["L0_ffn_b1"].reshape(E * IC, P).T,
        "w2": a["L0_ffn_w2"].reshape(E, IC, P, D).transpose(2, 0, 1, 3),
        "b2": a["L0_ffn_b2"].reshape(E * D),
        "wr": a["L0_ffn_wr"].reshape(KD, P, E).transpose(1, 0, 2),
        "br": a["L0_ffn_br"],
    }
    arrays = {f"in_{k}": _np.ascontiguousarray(v) for k, v in arrays.items()}
    nc = _bacc.Bacc("TRN2", target_bir_lowering=False, num_devices=1)
    args = [nc.dram_tensor(k, v.shape, mybir.dt.from_np(v.dtype), kind="ExternalInput").ap() for k, v in arrays.items()]
    out = nc.dram_tensor("out", _OUT, F32, kind="ExternalOutput").ap()
    attention_and_experts(nc, *args, out.rearrange("b n d -> (b n) d"))
    r = _run(nc, [arrays], core_ids=[0])
    return r.results[0]["out"]
```

```python
from contextlib import ExitStack

import numpy as np

import concourse.bass as bass
from concourse import mybir

F32 = mybir.dt.float32
F32R = mybir.dt.float32r
BF16 = mybir.dt.bfloat16
I32 = mybir.dt.int32
ALU = mybir.AluOpType
ACT = mybir.ActivationFunctionType
AX = mybir.AxisListType

P = 128
B, N, D = 8, 512, 256
H, FD, HD = 16, 16, 64
NT = N // P
KD = D // P
PAIRS = H // 2
PM = 4
NK = N + P
E, I = 8, 1024
TOK = B * N
TT = TOK // P
IC = I // P
SLOTS = TT + E - 1
CQ = float(1.0 / (4.0 * np.sqrt(2.0)))
HALF_ROOT = float(np.sqrt(0.5))
EPS_Z, EPS_LN = 1e-12, 1e-5
SKIP = 2 * TOK

BLOCKS = [(NT, 0, 0), (0, 0, 512), (1, 128, 1024), (3, 384, 1408), (2, 256, 1536)]
HALVES = [(0, 1024), (1024, 1792)]
XP = 8
ONES = 32
RING = 2
U_Q, U_K, U_KE, U_V, U_HEAD = 0, 1, 2, 3, 8
USES = U_HEAD + 2 * H


def attention_and_experts(nc, xT_in, x_in, wqk_in, wv_in, wo_in, w1_in, b1_in, w2_in, b2_in, wr_in, br_in, out):
    ybuf = nc.dram_tensor("attention_rows", [TOK + 1, D], F32).ap()
    with ExitStack() as ctx:
        def sem(name):
            return ctx.enter_context(nc.semaphore(name))

        logits = ctx.enter_context(nc.sbuf_tensor("logits", [P, TT, E], F32))
        ident = ctx.enter_context(nc.sbuf_tensor("ident", [P, P], F32))
        attention(nc, sem, xT_in, x_in, wqk_in, wv_in, wo_in, wr_in, br_in, ybuf, logits, ident)
        experts(nc, sem, w1_in, b1_in, w2_in, b2_in, ybuf, logits, ident, out)


def attention(nc, sem, xT_in, x_in, wqk_in, wv_in, wo_in, wr_in, br_in, ybuf, logits, ident):
    with ExitStack() as ctx:
        def sb(name, shape, dt=F32):
            return ctx.enter_context(nc.sbuf_tensor(name, shape, dt))

        def ps(name, shape):
            return ctx.enter_context(nc.psum_tensor(name, shape, F32))

        wqk_h, wqk_l = sb("wqk_h", [P, 3, KD, D], F32R), sb("wqk_l", [P, 3, KD, D], F32R)
        wv_h, wv_l = sb("wv_h", [P, 2, KD, I], F32R), sb("wv_l", [P, 2, KD, I], F32R)
        wo = sb("wo", [P, PAIRS, D])
        wr = sb("wr", [P, KD, E])
        br = sb("br", [P, E])
        xh, xl = sb("xh", [P, KD, N], F32R), sb("xl", [P, KD, N], F32R)
        qh, ql = sb("qh", [P, 2, N], F32R), sb("ql", [P, 2, N], F32R)
        kh, kl = sb("kh", [P, 2, NK], F32R), sb("kl", [P, 2, NK], F32R)
        qop = sb("qop", [P, RING, 2, N], F32R)
        kop = sb("kop", [P, RING, NK], F32R)
        raw = sb("raw", [P, 2, 1792])
        weights_h, weights_l = sb("weights_h", [P, 2, 1792], F32R), sb("weights_l", [P, 2, 1792], F32R)
        values_h = sb("values_h", [P, NT + 1, H, HD + ONES], F32R)
        values_l = sb("values_l", [P, NT + 1, H, HD], F32R)
        att = sb("att", [P, 2, N])
        denoms = sb("denoms", [P, 2, N])
        y = sb("y", [P, NT, D])
        xT = y[:, :, :].rearrange("p t d -> p (t d)").rearrange("p (k n) -> p k n", k=KD)
        xrow = raw[:, 1, 0:1024].rearrange("p (t d) -> p t d", t=NT)
        yT = sb("yT", [P, NT * KD, P])
        stats = sb("stats", [P, NT, 6])
        mv = sb("mv", [P, NT, 2])
        eps, minus_half = sb("y_eps", [P, 1]), sb("y_minus_half", [P, 1])
        rstd = sb("rstd", [P, NT])
        zrow = denoms[0:1, 0, 0:D]

        slot = [ps("slot0", [P, 1024]), ps("slot1", [P, 1024])]
        osum = [ps("osum0", [P, N]), ps("osum1", [P, N])]
        ysum = ps("ysum", [P, NT * D])

        w_loaded = [sem("w_loaded0"), sem("w_loaded1")]
        small_loaded = sem("small_loaded")
        w_split = sem("w_split")
        consts = sem("consts")
        zeroed = sem("zeroed")
        masks = sem("masks")
        xT_loaded, xrow_loaded = sem("xT_loaded"), sem("xrow_loaded")
        x_split = sem("x_split")
        slot_full = sem("slot_full")
        slot_free = [sem("slot_free0"), sem("slot_free1")]
        qk_hi, qk_lo = sem("qk_hi"), sem("qk_lo")
        op_ready = [sem(f"op_ready{i}") for i in range(RING)]
        v_hi = sem("v_hi")
        squared, masked, parts = sem("squared"), sem("masked"), sem("parts")
        w_hi = [sem("w_hi0"), sem("w_hi1")]
        o_full, copied, divided, att_used = sem("o_full"), sem("copied"), sem("divided"), sem("att_used")
        inverted = sem("inverted")
        y_step, rstd_step, y_ready = sem("y_step"), sem("rstd_step"), sem("y_ready")
        turned, yT_ready = sem("turned"), sem("yT_ready")
        logits_full, logits_read = sem("logits_full"), sem("logits_read")
        y_stored = sem("y_stored")
        pool_passed, dve_passed, sp_passed = sem("pool_passed"), sem("dve_passed"), sem("sp_passed")

        CHUNKS = [(0, 0), (0, 1), (0, 2), (1, 0), (1, 1), (1, 2), (1, 3)]
        STEPS = 1 + 2 * NT
        FREED = U_HEAD // 2

        def use(it, u):
            return it * USES + u

        def batches(eng, body):
            body(0, True, False)
            with eng.Fori(1, B - 1) as it:
                body(it, False, False)
            body(B - 1, False, True)

        block = ctx.enter_context(nc.Block())

        @block.sync
        def _(sp):
            sp.dma_start(xT[:, :, :], xT_in[0]).then_inc(xT_loaded, 16)
            for n, (kind, c) in enumerate(CHUNKS):
                if n >= 2:
                    sp.wait_ge(w_split, 2 * (n - 1))
                src = wqk_in[:, c, :] if kind == 0 else wv_in[:, c, :]
                sp.dma_start(raw[:, n % 2, 0:src.shape[1]], src).then_inc(w_loaded[n % 2], 16)
            sp.dma_start(wo[:, :, :], wo_in).then_inc(small_loaded, 16)
            sp.dma_start(wr[:, :, :], wr_in).then_inc(small_loaded, 16)
            sp.dma_start(br[:, :], br_in.partition_broadcast(P)).then_inc(small_loaded, 16)
            sp.wait_ge(zeroed, 2)
            sp.dma_start(ybuf[0:1, :], zrow).then_inc(small_loaded, 16)

            def body(it, first, last):
                sp.wait_ge(qk_hi, it * 3 + 3)
                sp.wait_ge(qk_lo, it * 3 + 3)
                for p in range(PAIRS):
                    m, r = p // PM, 32 * (p % PM)
                    if p >= RING:
                        sp.wait_ge(slot_full, use(it, U_HEAD + 4 * (p - RING) + 4))
                    elif not first:
                        sp.wait_ge(slot_full, use(it, U_HEAD + 4 * (p - RING + PAIRS) + 4) - USES)
                    for c in range(4):
                        sp.dma_start(kop[32 * c:32 * c + 32, p % RING, :].bitcast(F32),
                                     (kh, kl, kh, kl)[c][r:r + 32, m, :].bitcast(F32)).then_inc(op_ready[p % RING], 16)
                        for s in range(0, 32, FD):
                            sp.dma_start(qop[32 * c + s:32 * c + s + FD, p % RING, s // FD, :].bitcast(F32),
                                         (qh, ql, ql, qh)[c][r + s:r + s + FD, m, :].bitcast(F32))\
                                .then_inc(op_ready[p % RING], 16)
                    if p == 1 and not first:
                        store(it - 1)
                    if p == 2 and not last:
                        if not first:
                            sp.wait_ge(y_stored, it * 16)
                            sp.sem_inc(sp_passed, 1)
                            sp.wait_ge(turned, it)
                        sp.dma_start(xT[:, :, :], xT_in[it + 1]).then_inc(xT_loaded, 16)

                sp.wait_ge(parts, it * (2 * H) + 2 * H)
                sp.dma_start(xrow[:, :, :], x_in[it]).then_inc(xrow_loaded, 16)

            def store(it):
                sp.wait_ge(y_ready, it * NT + NT)
                sp.dma_start(ybuf[1:TOK + 1, :].rearrange("(b t p) d -> b p t d", p=P, t=NT)[it],
                             y[:, :, :]).then_inc(y_stored, 16)

            batches(sp, body)
            store(B - 1)
            sp.wait_ge(y_stored, 16 * B)
            sp.wait_ge(small_loaded, 64)

        @block.gpsimd
        def _(pool):
            pool.memset(zrow, 0.0).then_inc(zeroed, 1)
            pool.memset(qop[:, :, :, :].bitcast(F32), 0.0).then_inc(zeroed, 1)
            pool.memset(ident[:, :], 0.0).then_inc(masks, 1)
            pool.memset(values_h[:, :, :, HD:HD + ONES].bitcast(F32), 1.0).then_inc(consts, 1)
            pool.memset(eps[:, :], EPS_LN).then_inc(masks, 1)
            pool.memset(minus_half[:, :], -0.5).then_inc(masks, 1)
            pool.wait_ge(masks, 3)
            pool.affine_select(out=ident[:, :], in_=ident[:, :], compare_op=ALU.not_equal, fill=1.0, base=0,
                               pattern=[[-1, P]], channel_multiplier=1).then_inc(consts, 1)

            def split_x(b, n):
                if n == 0:
                    pool.wait_ge(xT_loaded, b * 16 + 16)
                    pool.sem_inc(pool_passed, 1)
                    if not (isinstance(b, int) and b == 0):
                        pool.wait_ge(slot_full, use(b, U_HEAD) - USES)
                        pool.sem_inc(pool_passed, 1)
                k, c = n * KD // XP, n % (XP // KD) * (KD * N // XP)
                cols = slice(c, c + KD * N // XP)
                pool.tensor_copy(xh[:, k, cols], xT[:, k, cols]).then_inc(x_split, 1)
                pool.wait_ge(x_split, b * (2 * XP) + (2 * n + 1))
                pool.tensor_tensor(xl[:, k, cols], xT[:, k, cols], xh[:, k, cols].bitcast(F32),
                                   ALU.subtract).then_inc(x_split, 1)

            for n in range(XP):
                split_x(0, n)

            def deviation(b):
                pool.wait_ge(y_step, b * STEPS + STEPS)
                pool.tensor_tensor(rstd[:, :], mv[:, :, 1], eps[:, :].to_broadcast([P, NT]),
                                   ALU.add).then_inc(rstd_step, 1)
                pool.wait_ge(rstd_step, b * 2 + 1)
                pool.tensor_tensor(rstd[:, :], rstd[:, :], minus_half[:, :].to_broadcast([P, NT]),
                                   ALU.pow).then_inc(rstd_step, 1)

            def body(it, first, last):
                def cut(k, a, blocks):
                    w = raw[:, k, a:a + blocks * P].rearrange("p (b c) -> p b c", b=blocks)
                    pool.affine_select(out=w, in_=w, compare_op=ALU.is_ge, fill=-0.5, base=0,
                                       pattern=[[0, blocks], [1, P]], channel_multiplier=-1).then_inc(masked, 1)

                def divide(p):
                    pool.wait_ge(inverted, it * PAIRS + (p + 1))
                    pool.tensor_tensor(att[:, p % 2, :], att[:, p % 2, :], denoms[:, p % 2, :],
                                       ALU.mult).then_inc(divided, 1)

                if not first:
                    deviation(it - 1)
                for h in range(H):
                    pool.wait_ge(squared, it * (2 * H) + (2 * h + 1))
                    pool.sem_inc(pool_passed, 1)
                    cut(h % 2, 512, 1)
                    if h >= 5 and h % 2 == 1:
                        divide((h - 5) // 2)
                    pool.wait_ge(squared, it * (2 * H) + (2 * h + 2))
                    pool.sem_inc(pool_passed, 1)
                    cut(h % 2, 1024, 1)
                    cut(h % 2, 1408, 2)
                    if 6 <= h < 6 + XP and not last:
                        split_x(it + 1, h - 6)
                divide(PAIRS - 2)
                divide(PAIRS - 1)

            batches(pool, body)
            deviation(B - 1)

        @block.scalar
        def _(act):
            def body(it, first, last):
                def square(h, half):
                        a, b = HALVES[half]
                        u = U_HEAD + 2 * h + half
                        act.wait_ge(slot_full, use(it, u) + 1)
                        if h >= 2 or not first:
                            act.wait_ge(parts, it * (2 * H) + (2 * h - 3 + half))
                        act.activation(raw[:, h % 2, a:b], slot[half][:, 0:b - a], ACT.Square,
                                       bias=HALF_ROOT).then_inc(squared, 1)

                def high_weights(h):
                    a, b = HALVES[1]
                    act.wait_ge(masked, it * (3 * H) + (3 * h + 3))
                    if h >= 2 or not first:
                        act.wait_ge(o_full, it * H + (h - 1))
                    act.activation(weights_h[:, h % 2, a:b], raw[:, h % 2, a:b], ACT.Identity,
                                   bias=0.5).then_inc(w_hi[1], 1)

                def copy_sums(h):
                    p, r = h // 2, HD * (h % 2)
                    act.wait_ge(o_full, it * H + (h + 1))
                    if p >= 2 or not first:
                        act.wait_ge(att_used, it * PAIRS + (p - 1))
                    act.activation(att[r:r + HD, p % 2, :], osum[h % 2][0:HD, :], ACT.Copy).then_inc(copied, 1)
                    for o in range(0, HD, ONES):
                        act.activation(denoms[r + o:r + o + ONES, p % 2, :], osum[h % 2][HD:HD + ONES, :],
                                       ACT.Identity, bias=EPS_Z).then_inc(copied, 1)

                act.wait_ge(slot_full, use(it, U_Q) + 1)
                act.activation(qh[:, :, :], slot[0][:, :].rearrange("p (m n) -> p m n", m=2), ACT.Copy,
                               scale=CQ).then_inc(qk_hi, 1)
                act.wait_ge(slot_full, use(it, U_K) + 1)
                act.activation(kh[:, :, 0:N], slot[1][:, :].rearrange("p (m n) -> p m n", m=2),
                               ACT.Copy).then_inc(qk_hi, 1)
                act.wait_ge(slot_full, use(it, U_KE) + 1)
                act.activation(kh[:, :, N:NK], slot[0][:, 0:2 * P].rearrange("p (m n) -> p m n", m=2),
                               ACT.Copy).then_inc(qk_hi, 1)
                for t in range(NT + 1):
                    act.wait_ge(slot_full, use(it, U_V + t) + 1)
                    if t == 0 and not first:
                        act.wait_ge(o_full, it * H)
                    act.activation(values_h[:, t, :, 0:HD],
                                   slot[(U_V + t) % 2][:, :].rearrange("p (h d) -> p h d", h=H),
                                   ACT.Copy).then_inc(v_hi, 1)
                for h in range(H):
                    if h >= 3:
                        copy_sums(h - 3)
                    square(h, 0)
                    if h >= 1:
                        high_weights(h - 1)
                    square(h, 1)
                copy_sums(H - 3)
                high_weights(H - 1)
                copy_sums(H - 2)
                copy_sums(H - 1)

            batches(act, body)

        @block.vector
        def _(dve):
            for n, (kind, c) in enumerate(CHUNKS):
                hi, lo = (wqk_h, wqk_l) if kind == 0 else (wv_h, wv_l)
                if kind == 0:
                    hi, lo = hi[:, c, :, :].rearrange("p k n -> p (k n)"), lo[:, c, :, :].rearrange("p k n -> p (k n)")
                else:
                    hi, lo = hi[:, c // 2, c % 2, :], lo[:, c // 2, c % 2, :]
                src = raw[:, n % 2, 0:hi.shape[1]]
                dve.wait_ge(w_loaded[n % 2], 16 * (n // 2 + 1))
                dve.tensor_copy(hi, src).then_inc(w_split, 1)
                dve.wait_ge(w_split, 2 * n + 1)
                dve.tensor_tensor(lo, src, hi.bitcast(F32), ALU.subtract).then_inc(w_split, 1)

            def body(it, first, last):
                def low(dst, src, factor, hi, n, free):
                    dve.wait_ge(qk_hi, it * 3 + n)
                    dve.scalar_tensor_tensor(dst, src, factor, hi.bitcast(F32), ALU.mult, ALU.subtract).then_inc(qk_lo, 1)
                    dve.wait_ge(qk_lo, it * 3 + n)
                    dve.sem_inc(slot_free[free], 1)

                def low_values(t):
                    dve.wait_ge(v_hi, it * (NT + 1) + (t + 1))
                    u = U_V + t
                    dve.tensor_tensor(values_l[:, t, :, :], slot[u % 2][:, :].rearrange("p (h d) -> p h d", h=H),
                                      values_h[:, t, :, 0:HD].bitcast(F32), ALU.subtract).then_inc(slot_free[u % 2], 1)

                def split_weights(h, k):
                        a, b = HALVES[k]
                        src = raw[:, h % 2, a:b]
                        if k == 0:
                            dve.wait_ge(masked, it * (3 * H) + (3 * h + 1))
                            if h >= 2 or not first:
                                dve.wait_ge(o_full, it * H + (h - 1))
                            dve.tensor_scalar(weights_h[:, h % 2, a:b], src, 0.5, None, ALU.add).then_inc(w_hi[0], 1)
                        dve.wait_ge(w_hi[k], it * H + (h + 1))
                        dve.scalar_tensor_tensor(weights_l[:, h % 2, a:b], src, 0.5,
                                                 weights_h[:, h % 2, a:b].bitcast(F32), ALU.add,
                                                 ALU.subtract).then_inc(parts, 1)

                m2 = "p (m n) -> p m n"
                low(ql[:, :, :], slot[0][:, :].rearrange(m2, m=2), CQ, qh[:, :, :], 1, 0)
                low(kl[:, :, 0:N], slot[1][:, :].rearrange(m2, m=2), 1.0, kh[:, :, 0:N], 2, 1)
                low(kl[:, :, N:NK], slot[0][:, 0:2 * P].rearrange(m2, m=2), 1.0, kh[:, :, N:NK], 3, 0)
                if not first:
                    invert(it - 1, PAIRS - 1)
                low_values(0)
                low_values(1)
                if not first:
                    residual(it - 1)
                    moments(it - 1)
                low_values(2)
                if not first:
                    normalise(it - 1)
                low_values(3)
                if not first:
                    turned_rows(it - 1)
                low_values(4)
                if not first:
                    logits_of(it - 1)
                for h in range(H):
                    split_weights(h, 0)
                    if h >= 3 and h % 2 == 1:
                        invert(it, (h - 3) // 2)
                    split_weights(h, 1)

            def invert(b, p):
                dve.wait_ge(copied, b * (3 * H) + (6 * p + 6))
                dve.reciprocal(denoms[:, p % 2, :], denoms[:, p % 2, :]).then_inc(inverted, 1)

            def residual(b):
                dve.wait_ge(att_used, b * PAIRS + PAIRS)
                dve.wait_ge(xrow_loaded, b * 16 + 16)
                if not (isinstance(b, int) and b == 0):
                    dve.wait_ge(y_stored, b * 16)
                dve.tensor_tensor(y[:, :, :], ysum[:, :].rearrange("p (t d) -> p t d", t=NT), xrow[:, :, :],
                                  ALU.add).then_inc(y_step, 1)

            def moments(b):
                dve.wait_ge(y_step, b * STEPS + 1)
                for t in range(NT):
                    dve.bn_stats(stats[:, t, :], y[:, t, :]).then_inc(y_step, 1)
                dve.wait_ge(y_step, b * STEPS + (1 + NT))
                dve.sem_inc(dve_passed, 1)
                for t in range(NT):
                    dve.bn_aggr(mv[:, t, :], stats[:, t, :]).then_inc(y_step, 1)

            def normalise(b):
                dve.wait_ge(rstd_step, b * 2 + 2)
                for t in range(NT):
                    dve.tensor_scalar(y[:, t, :], y[:, t, :], mv[:, t, 0:1], rstd[:, t:t + 1], ALU.subtract,
                                      ALU.mult).then_inc(y_ready, 1)

            def turned_rows(b):
                dve.wait_ge(turned, b + 1)
                for k in range(2):
                    dve.tensor_copy(yT[:, 4 * k:4 * k + 4, :],
                                    osum[k][:, :].rearrange("p (t n) -> p t n", n=P)).then_inc(yT_ready, 1)

            def logits_of(b):
                dve.wait_ge(logits_full, b + 1)
                dve.tensor_tensor(logits[:, bass.ts(b, NT), :], osum[1][:, 0:NT * E].rearrange("p (t e) -> p t e", e=E),
                                  br[:, :].unsqueeze(1).to_broadcast([P, NT, E]), ALU.add).then_inc(logits_read, 1)

            batches(dve, body)
            invert(B - 1, PAIRS - 1)
            residual(B - 1)
            moments(B - 1)
            normalise(B - 1)
            turned_rows(B - 1)
            logits_of(B - 1)

        @block.tensor
        def _(pe):
            def three(dst, wh, wl, vh, vl):
                parts = [(wh, vh), (wh, vl), (wl, vh)]
                for n, (a, b) in enumerate((a, b) for a in range(3) for b in range(KD)):
                    last = pe.matmul(dst, parts[a][0](b), parts[a][1](b), start=(n == 0), stop=(n == 3 * KD - 1))
                return last

            def take(it, u):
                if u >= 2:
                    pe.wait_ge(slot_free[u % 2], it * FREED + u // 2)
                elif not (isinstance(it, int) and it == 0):
                    pe.wait_ge(squared, it * (2 * H))

            def turn_rows(b):
                pe.wait_ge(y_ready, b * NT + NT)
                pe.wait_ge(copied, b * (3 * H) + 3 * H)
                for t in range(NT):
                    for k in range(KD):
                        n = t * KD + k
                        last = pe.transpose(osum[n // 4][:, n % 4 * P:n % 4 * P + P], y[:, t, k * P:(k + 1) * P],
                                            ident[:, :])
                last.then_inc(turned, 1)

            def router(b):
                pe.wait_ge(yT_ready, b * 2 + 2)
                for t in range(NT):
                    for k in range(KD):
                        last = pe.matmul(osum[1][:, t * E:(t + 1) * E], yT[:, t * KD + k, :], wr[:, k, :],
                                         start=(k == 0), stop=(k == KD - 1))
                last.then_inc(logits_full, 1)

            def output(it, p):
                pe.wait_ge(divided, it * PAIRS + (p + 1))
                if p == 0 and not (isinstance(it, int) and it == 0):
                    pe.wait_ge(y_step, it * STEPS - (STEPS - 1))
                for t in range(NT):
                    last = pe.matmul(ysum[:, t * D:(t + 1) * D], att[:, p % 2, t * P:(t + 1) * P], wo[:, p, :],
                                     start=(p == 0 and t % 2 == 0), stop=(p == PAIRS - 1), skip_group_check=True)
                    if t == NT - 1:
                        last.then_inc(att_used, 1)

            def body(it, first, last_batch):
                def project_qk(u, w, cols, sl):
                    take(it, u)
                    for m in range(2):
                        lo, hi = m * P, (m + 1) * P
                        last = three(slot[sl][:, m * cols:(m + 1) * cols],
                                     lambda k: wqk_h[:, w, k, lo:hi], lambda k: wqk_l[:, w, k, lo:hi],
                                     lambda k: xh[:, k, 0:cols], lambda k: xl[:, k, 0:cols])
                    last.then_inc(slot_full, 1)

                def project_values(t):
                    u, enc = U_V + t, int(t == NT)
                    a = 0 if enc else t * P
                    take(it, u)
                    for c in range(2):
                        last = three(slot[u % 2][:, c * 512:(c + 1) * 512],
                                     lambda k: xh[:, k, a:a + P], lambda k: xl[:, k, a:a + P],
                                     lambda k: wv_h[:, enc, k, c * 512:(c + 1) * 512],
                                     lambda k: wv_l[:, enc, k, c * 512:(c + 1) * 512])
                    last.then_inc(slot_full, 1)

                def scores(h, half):
                    p = h // 2
                    if h % 2 == 0 and half == 0:
                        pe.wait_ge(op_ready[p % RING], it * (192 * PAIRS // RING) + 192 * (p // RING + 1))
                    if h == 0:
                        pe.wait_ge(slot_free[half], it * FREED + FREED)
                    else:
                        pe.wait_ge(squared, it * (2 * H) + (2 * h + half - 1))
                    off = HALVES[half][0]
                    for j, q0, col in BLOCKS[2 * half:2 * half + 2 + half]:
                        k0 = j * P
                        last = pe.matmul(slot[half][:, col - off:col - off + N - q0], kop[:, p % RING, k0:k0 + P],
                                         qop[:, p % RING, h % 2, q0:N], start=True, stop=True)
                    last.then_inc(slot_full, 1)

                def weigh(h, half):
                    pe.wait_ge(parts, it * (2 * H) + (2 * h + half + 1))
                    if half == 0 and (h >= 2 or not first):
                        pe.wait_ge(copied, it * (3 * H) + (3 * h - 3))
                    if half == 0 and h == 1 and not first:
                        pe.wait_ge(logits_read, it)
                    for n, (j, q0, col) in enumerate(BLOCKS[2 * half:2 * half + 2 + half]):
                        vh = values_h[:, j, h, :]
                        wh, wl = weights_h[:, h % 2, col:col + N - q0], weights_l[:, h % 2, col:col + N - q0]
                        dst = osum[h % 2][0:HD + ONES, :]
                        pe.matmul(dst[:, q0:N], vh, wh, start=(half == 0 and n == 0), stop=False)
                        pe.matmul(dst[0:HD, q0:N], values_l[:, j, h, :], wh, start=False, stop=False)
                        last = pe.matmul(dst[:, q0:N], vh, wl, start=False, stop=(half == 1 and n == 2))
                    if half == 1:
                        last.then_inc(o_full, 1)

                if first:
                    pe.wait_ge(w_split, 6)
                pe.wait_ge(x_split, it * (2 * XP) + 2 * XP)
                project_qk(U_Q, 0, N, 0)
                project_qk(U_K, 1, N, 1)
                project_qk(U_KE, 2, P, 0)
                if first:
                    pe.wait_ge(w_split, 2 * len(CHUNKS))
                    pe.wait_ge(small_loaded, 64)
                    pe.wait_ge(consts, 2)
                for t in range(NT + 1):
                    project_values(t)
                    if t == 1 and not first:
                        last_output(it - 1)
                    if t == NT - 1 and not first:
                        turn_rows(it - 1)
                scores(0, 0)
                if not first:
                    router(it - 1)
                scores(0, 1)
                scores(1, 0)
                for h in range(H):
                    if h + 1 < H:
                        scores(h + 1, 1)
                    weigh(h, 0)
                    if h + 2 < H:
                        scores(h + 2, 0)
                    if h >= 4 and h % 2 == 0:
                        output(it, h // 2 - 2)
                    weigh(h, 1)

            def last_output(b):
                output(b, PAIRS - 2)
                output(b, PAIRS - 1)

            batches(pe, body)
            last_output(B - 1)
            turn_rows(B - 1)
            router(B - 1)


def experts(nc, sem, w1_in, b1_in, w2_in, b2_in, ybuf, logits, ident, out):
    with ExitStack() as ctx:
        def sb(name, shape, dt=F32):
            return ctx.enter_context(nc.sbuf_tensor(name, shape, dt))

        def ps(name, shape):
            return ctx.enter_context(nc.psum_tensor(name, shape, F32))

        w1 = sb("w1", [P, E, KD, I])
        w2 = sb("w2", [P, E, IC, D])
        b1 = sb("b1", [P, E * IC])
        b2 = sb("b2", [P, E * D])
        row_index = sb("row_index", [P, SLOTS], I32)
        out_index = sb("out_index", [P, SLOTS], I32)
        gates = sb("gates", [P, SLOTS])
        expert_of = sb("expert_of", [P, SLOTS], I32)

        w_seq = sem("expert_weights")
        table_loaded = sem("table_loaded")
        w_sem = [sem("expert_loaded0"), sem("expert_loaded1")]
        routed = sem("routed")

        with ExitStack() as inner:
            route(nc, inner, sem, w_seq, table_loaded, w_sem, routed, w1, w2, b1, b2, w1_in, w2_in, b1_in, b2_in,
                  logits, row_index, out_index, gates, expert_of)
        run_experts(nc, ctx, sem, w_seq, w1, w2, b1, b2, row_index, out_index, gates, expert_of,
                    ybuf, ident, out, w_sem, w1_in, w2_in)


LOADED_EARLY = 2


def load_expert(sp, e, w1, w2, w1_in, w2_in, w_sem):
    sp.dma_start(w1[:, e, :, :], w1_in[:, e, :, :]).then_inc(w_sem[e % 2], 16)
    sp.dma_start(w2[:, e, :, :], w2_in[:, e, :, :]).then_inc(w_sem[e % 2], 16)


def route(nc, ctx, sem, w_seq, table_loaded, w_sem, routed, w1, w2, b1, b2, w1_in, w2_in, b1_in, b2_in,
          logits, row_index, out_index, gates, expert_of):
    def sb(name, shape, dt=F32):
        return ctx.enter_context(nc.sbuf_tensor(name, shape, dt))

    def ps(name, shape):
        return ctx.enter_context(nc.psum_tensor(name, shape, F32))

    falling = sb("falling", [P, E])
    tile_starts = sb("tile_starts", [P, TT])
    count128 = sb("count128", [P, P])
    token1 = sb("token1", [P, TT])
    before = sb("before", [P, P], BF16)
    ones = sb("ones", [P, P], BF16)
    ones32 = sb("ones32", [P, TT])
    top = sb("top", [P, TT])
    second = sb("second", [P, TT])
    key = sb("key", [P, TT, E])
    hot = sb("hot", [P, TT, E])
    hotb = sb("hotb", [P, TT, E], BF16)
    rest = sb("rest", [P, TT, E])
    gate = sb("gate", [P, TT])
    kmax = sb("kmax", [P, TT])
    cum = sb("cum", [P, E, TT])
    more = sb("more", [P, E, TT])
    used = sb("used", [P, E])
    last_slot = sb("last_slot", [P, E])
    first_row = sb("first_row", [P, E])
    place = sb("place", [P, TT, E])
    pos = sb("pos", [P, TT])
    pos_i = sb("pos_i", [P, TT], I32)
    slot_i = sb("slot_i", [P, TT], I32)
    row_i = sb("row_i", [P, TT], I32)
    slot_f = sb("slot_f", [P, TT])
    row_f = sb("row_f", [P, TT])
    in_slot = sb("in_slot", [P, TT, SLOTS])
    carried = sb("carried", [P, TT, 2, SLOTS])
    in_row = sb("in_row", [P, TT, P])
    passed = sb("passed", [P, SLOTS, E - 1])
    expert_f = sb("expert_f", [P, SLOTS])
    index_f = sb("index_f", [P, SLOTS])
    empty = sb("empty", [P, SLOTS])
    ranks = ps("ranks", [P, TT * E])
    totals = ps("totals", [P, TT * E])
    found = ps("found", [P, 2 * SLOTS])

    made = sem("route_consts")
    step = sem("route_step")
    counted = sem("counted")
    exp_in, exp_out = sem("exp_in"), sem("exp_out")
    placed = sem("placed")
    found_all = sem("found_all")

    block = ctx.enter_context(nc.Block())

    @block.sync
    def _(sp):
        sp.dma_start(b1[:, :], b1_in).then_inc(table_loaded, 16)
        sp.dma_start(b2[:, :], b2_in.partition_broadcast(P)).then_inc(table_loaded, 16)
        for e in range(LOADED_EARLY):
            load_expert(sp, e, w1, w2, w1_in, w2_in, w_sem)
        sp.wait_ge(table_loaded, 32)

    @block.gpsimd
    def _(pool):
        pool.iota(falling[:, :], [[-1, E]], base=E, channel_multiplier=0,
                  allow_small_or_imprecise_dtypes=True).then_inc(made, 1)
        pool.iota(tile_starts[:, :], [[P, TT]], base=0, channel_multiplier=0,
                  allow_small_or_imprecise_dtypes=True).then_inc(made, 1)
        pool.iota(count128[:, :], [[1, P]], base=0, channel_multiplier=0,
                  allow_small_or_imprecise_dtypes=True).then_inc(made, 1)
        pool.iota(token1[:, :], [[P, TT]], base=1, channel_multiplier=1,
                  allow_small_or_imprecise_dtypes=True).then_inc(made, 1)
        pool.memset(ones32[:, :], 1.0).then_inc(made, 1)
        pool.memset(ones[:, :], 1.0).then_inc(made, 1)
        pool.memset(before[:, :], 1.0).then_inc(made, 1)
        pool.wait_ge(made, 7)
        pool.affine_select(out=before[:, :], in_=before[:, :], compare_op=ALU.is_gt, fill=0.0, base=0,
                           pattern=[[1, P]], channel_multiplier=-1).then_inc(made, 1)

    @block.scalar
    def _(act):
        act.wait_ge(exp_in, 1)
        act.activation(gate[:, :], second[:, :], ACT.Exp).then_inc(exp_out, 1)

    @block.tensor
    def _(pe):
        pe.wait_ge(made, 8)
        pe.wait_ge(counted, 1)
        flat = hotb[:, :, :].rearrange("p t e -> p (t e)")
        pe.matmul(ranks[:, :], before[:, :], flat, start=True, stop=True)
        pe.matmul(totals[:, :], ones[:, :], flat, start=True, stop=True).then_inc(counted, 1)
        pe.wait_ge(placed, 1)
        for t in range(TT):
            last = pe.matmul(found[:, :], in_row[:, t, :], carried[:, t, :, :].rearrange("p a s -> p (a s)"),
                             start=(t == 0), stop=(t == TT - 1))
        last.then_inc(found_all, 1)

    @block.vector
    def _(dve):
        n = [0]

        def after(op):
            n[0] += 1
            op.then_inc(step, 1)
            dve.wait_ge(step, n[0])

        def over_e(ap):
            return ap.unsqueeze(2).to_broadcast([P, TT, E])

        def over_t(ap):
            return ap.unsqueeze(1).to_broadcast([P, TT, E])

        dve.wait_ge(made, 8)
        after(dve.tensor_reduce(top[:, :], logits[:, :, :], AX.X, ALU.max))
        after(dve.tensor_tensor(key[:, :, :], logits[:, :, :], over_e(top[:, :]), ALU.is_ge))
        after(dve.tensor_tensor(key[:, :, :], key[:, :, :], over_t(falling[:, :]), ALU.mult))
        after(dve.tensor_reduce(kmax[:, :], key[:, :, :], AX.X, ALU.max))
        after(dve.tensor_tensor(hot[:, :, :], over_t(falling[:, :]), over_e(kmax[:, :]), ALU.is_equal))
        after(dve.tensor_copy(hotb[:, :, :], hot[:, :, :]))
        dve.sem_inc(counted, 1)
        after(dve.scalar_tensor_tensor(rest[:, :, :], hot[:, :, :], -3.0e38, logits[:, :, :], ALU.mult, ALU.add))
        after(dve.tensor_reduce(second[:, :], rest[:, :, :], AX.X, ALU.max))
        after(dve.tensor_tensor(second[:, :], second[:, :], top[:, :], ALU.subtract))
        dve.sem_inc(exp_in, 1)
        dve.wait_ge(counted, 2)
        by_tile = totals[:, :].rearrange("p (t e) -> p t e", e=E)
        for e in range(E):
            op = dve.tensor_tensor_scan(cum[:, e, :], ones32[:, :], by_tile[:, :, e], 0.0, ALU.mult, ALU.add)
            if e < E - 1:
                n[0] += 1
                op.then_inc(step, 1)
        after(op)
        after(dve.tensor_tensor(more[:, :, :], cum[:, :, TT - 1:TT].to_broadcast([P, E, TT]),
                                tile_starts[:, :].unsqueeze(1).to_broadcast([P, E, TT]), ALU.is_gt))
        after(dve.tensor_reduce(used[:, :], more[:, :, :], AX.X, ALU.add))
        after(dve.tensor_scalar(used[:, :], used[:, :], 1.0, None, ALU.max))
        after(dve.tensor_tensor_scan(last_slot[:, :], ones32[:, 0:E], used[:, :], 0.0, ALU.mult, ALU.add))
        after(dve.tensor_tensor(first_row[:, :], last_slot[:, :], used[:, :], ALU.subtract))
        after(dve.tensor_scalar(first_row[:, :], first_row[:, :], float(P), None, ALU.mult))
        after(dve.tensor_tensor(place[:, :, :], cum[:, :, :].rearrange("p e t -> p t e"), by_tile, ALU.subtract))
        after(dve.tensor_tensor(place[:, :, :], place[:, :, :], ranks[:, :].rearrange("p (t e) -> p t e", e=E),
                                ALU.add))
        after(dve.tensor_tensor(place[:, :, :], place[:, :, :], over_t(first_row[:, :]), ALU.add))
        after(dve.tensor_tensor(place[:, :, :], place[:, :, :], hot[:, :, :], ALU.mult))
        after(dve.tensor_reduce(pos[:, :], place[:, :, :], AX.X, ALU.add))
        after(dve.tensor_copy(pos_i[:, :], pos[:, :]))
        after(dve.tensor_scalar(slot_i[:, :], pos_i[:, :], 7, None, ALU.logical_shift_right))
        after(dve.tensor_scalar(row_i[:, :], pos_i[:, :], P - 1, None, ALU.bitwise_and))
        after(dve.tensor_copy(slot_f[:, :], slot_i[:, :]))
        after(dve.tensor_copy(row_f[:, :], row_i[:, :]))
        after(dve.tensor_tensor(in_row[:, :, :], count128[:, :].unsqueeze(1).to_broadcast([P, TT, P]),
                                row_f[:, :].unsqueeze(2).to_broadcast([P, TT, P]), ALU.is_equal))
        after(dve.tensor_tensor(in_slot[:, :, :], count128[:, 0:SLOTS].unsqueeze(1).to_broadcast([P, TT, SLOTS]),
                                slot_f[:, :].unsqueeze(2).to_broadcast([P, TT, SLOTS]), ALU.is_equal))
        dve.wait_ge(exp_out, 1)
        after(dve.tensor_scalar(gate[:, :], gate[:, :], 1.0, None, ALU.add))
        after(dve.reciprocal(gate[:, :], gate[:, :]))
        after(dve.tensor_tensor(carried[:, :, 0, :], in_slot[:, :, :],
                                token1[:, :].unsqueeze(2).to_broadcast([P, TT, SLOTS]), ALU.mult))
        after(dve.tensor_tensor(carried[:, :, 1, :], in_slot[:, :, :],
                                gate[:, :].unsqueeze(2).to_broadcast([P, TT, SLOTS]), ALU.mult))
        dve.sem_inc(placed, 1)
        after(dve.tensor_tensor(passed[:, :, :], count128[:, 0:SLOTS].unsqueeze(2).to_broadcast([P, SLOTS, E - 1]),
                                last_slot[:, 0:E - 1].unsqueeze(1).to_broadcast([P, SLOTS, E - 1]), ALU.is_ge))
        after(dve.tensor_reduce(expert_f[:, :], passed[:, :, :], AX.X, ALU.add))
        after(dve.tensor_copy(expert_of[:, :], expert_f[:, :]))
        dve.wait_ge(found_all, 1)
        after(dve.tensor_copy(row_index[:, :], found[:, 0:SLOTS]))
        after(dve.tensor_copy(gates[:, :], found[:, SLOTS:2 * SLOTS]))
        after(dve.tensor_scalar(empty[:, :], found[:, 0:SLOTS], 0.0, float(SKIP + 1), ALU.is_equal, ALU.mult))
        after(dve.scalar_tensor_tensor(index_f[:, :], found[:, 0:SLOTS], -1.0, empty[:, :], ALU.add, ALU.add))
        after(dve.tensor_copy(out_index[:, :], index_f[:, :]))
        dve.sem_inc(routed, 1)


def run_experts(nc, ctx, sem, w_seq, w1, w2, b1, b2, row_index, out_index, gates, expert_of,
                ybuf, ident, out, w_sem, w1_in, w2_in):
    RING = 4
    UNROLL = 4
    PEELED = 3

    def sb(name, shape, dt=F32):
        return ctx.enter_context(nc.sbuf_tensor(name, shape, dt))

    def ps(name, shape):
        return ctx.enter_context(nc.psum_tensor(name, shape, F32))

    rows = sb("rows", [P, RING, D])
    rows_col = sb("rows_col", [P, RING], I32)
    out_col = sb("out_col", [P, 2], I32)
    rowsT = sb("rowsT", [P, 2, KD, P])
    inner = sb("inner", [P, 2, I])
    active = sb("active", [P, 2, IC, P])
    result = sb("result", [P, 2, D])
    centred = sb("centred", [P, 2, D])
    final = sb("final", [P, 2, D])
    stats = sb("e_stats", [P, 2, 6])
    mv = sb("e_mv", [P, 2, 2])
    rs = sb("e_rs", [P, 2])
    eps = sb("eps", [P, 1])
    minus_half = sb("minus_half", [P, 1])

    turned = ps("turned", [P, KD * P])
    up = ps("up", [P, I])
    upT = ps("upT", [P, I])
    down = [ps("down0", [P, D]), ps("down1", [P, D])]

    gathered = [sem(f"gathered{i}") for i in range(RING)]
    indexed, ready_consts = sem("indexed"), sem("loop_consts")
    turned_full, rowsT_ready = sem("turned_full"), sem("rowsT_ready")
    up_full, inner_ready = sem("up_full"), sem("inner_ready")
    upT_full, active_ready = sem("upT_full"), sem("active_ready")
    down_full, down_read = sem("down_full"), sem("down_read")
    norm_step, final_step = sem("norm_step"), sem("final_step")
    scattered = [sem("scattered0"), sem("scattered1")]
    passed, dve_passed = sem("loop_passed"), sem("loop_dve_passed")
    NORM = 4
    FINAL = 4

    def steps(eng, body):
        for s in range(PEELED):
            body(s, s)
        loops = (SLOTS - PEELED - 1) // UNROLL
        with eng.Fori(0, loops) as i:
            for j in range(UNROLL):
                body(i * UNROLL + (PEELED + j), PEELED + j)
        for s in range(PEELED + loops * UNROLL, SLOTS):
            body(s, s)

    def expert(eng, s):
        return eng.value_load(expert_of[0:1, bass.ds(s, 1)], min_val=0, max_val=E - 1)

    block = ctx.enter_context(nc.Block())

    @block.sync
    def _(sp):
        for e in range(LOADED_EARLY, E):
            load_expert(sp, e, w1, w2, w1_in, w2_in, w_sem)
            sp.wait_ge(w_sem[(e - 1) % 2], 32 * ((e - 1) // 2 + 1))
            if e - 1 == LOADED_EARLY - 1:
                sp.sem_inc(w_seq, LOADED_EARLY)
            else:
                sp.sem_inc(w_seq, 1)
        sp.wait_ge(w_sem[(E - 1) % 2], 32 * ((E - 1) // 2 + 1))
        sp.sem_inc(w_seq, 1)

    @block.gpsimd
    def _(pool):
        pool.memset(eps[:, :], EPS_LN).then_inc(ready_consts, 1)
        pool.memset(minus_half[:, :], -0.5).then_inc(ready_consts, 1)
        pool.wait_ge(ready_consts, 2)

        def gather(s, k):
            pool.tensor_copy(rows_col[:, k % RING:k % RING + 1], row_index[:, bass.ds(s, 1)]).then_inc(indexed, 1)
            pool.wait_ge(indexed, s + 1)
            pool.sem_inc(passed, 1)
            pool.indirect_dma_start(rows[:, k % RING, :], None, ybuf[:, :],
                                    bass.IndirectOffsetOnAxis(ap=rows_col[:, k % RING:k % RING + 1], axis=0))\
                .then_inc(gathered[k % RING], 16)

        def finish(s, k):
            p = k % 2
            if not (isinstance(s, int) and s < 2):
                pool.wait_ge(scattered[p], (s - p) * 8)
                pool.sem_inc(passed, 1)
            pool.tensor_copy(out_col[:, p:p + 1], out_index[:, bass.ds(s, 1)]).then_inc(final_step, 1)
            pool.wait_ge(norm_step, s * NORM + NORM)
            pool.tensor_tensor(rs[:, p:p + 1], mv[:, p, 1:2], eps[:, :], ALU.add).then_inc(final_step, 1)
            pool.wait_ge(final_step, s * FINAL + 2)
            pool.tensor_tensor(rs[:, p:p + 1], rs[:, p:p + 1], minus_half[:, :], ALU.pow).then_inc(final_step, 1)
            pool.wait_ge(final_step, s * FINAL + 3)
            pool.tensor_tensor(final[:, p, :], centred[:, p, :], rs[:, p:p + 1].to_broadcast([P, D]),
                               ALU.mult).then_inc(final_step, 1)
            pool.wait_ge(final_step, s * FINAL + 4)
            pool.sem_inc(passed, 1)
            pool.indirect_dma_start(out, bass.IndirectOffsetOnAxis(ap=out_col[:, p:p + 1], axis=0), final[:, p, :],
                                    None, bounds_check=TOK - 1, oob_is_err=False).then_inc(scattered[p], 16)

        for s in range(3):
            gather(s, s)
        finish(0, 0)
        gather(3, 3)
        with pool.Fori(0, (SLOTS - 7) // UNROLL) as i:
            for j in range(UNROLL):
                gather(i * UNROLL + (4 + j), 4 + j)
                finish(i * UNROLL + (1 + j), 1 + j)
        for s in range(SLOTS - 6, SLOTS):
            if s + 3 < SLOTS:
                gather(s + 3, s + 3)
            finish(s, s)
        for p in range(2):
            pool.wait_ge(scattered[p], 16 * ((SLOTS + 1 - p) // 2))

    @block.scalar
    def _(act):
        def turn(s, k):
            act.wait_ge(turned_full, s + 1)
            if not (isinstance(s, int) and s < 2):
                act.wait_ge(up_full, s - 1)
            act.activation(rowsT[:, k % 2, :, :], turned[:, :].rearrange("p (k n) -> p k n", k=KD),
                           ACT.Copy).then_inc(rowsT_ready, 1)

        def body(s, k):
            if not (isinstance(s, int) and s == SLOTS - 1):
                turn(s + 1, k + 1)
            e = expert(act, s)
            act.wait_ge(upT_full, s + 1)
            if not (isinstance(s, int) and s < 2):
                act.wait_ge(down_full, s - 1)
            for c in range(IC):
                act.activation(active[:, k % 2, c, :], upT[:, c * P:(c + 1) * P], ACT.Gelu,
                               bias=b1[:, bass.ds(e * IC + c, 1)]).then_inc(active_ready, 1)

        turn(0, 0)
        steps(act, body)

    @block.vector
    def _(dve):
        def residual(s, k):
            p = k % 2
            e = expert(dve, s)
            dve.wait_ge(down_full, s + 1)
            if not (isinstance(s, int) and s < 2):
                dve.wait_ge(final_step, s * FINAL - FINAL)
            dve.tensor_tensor(result[:, p, :], down[p][:, :], b2[:, bass.ds(e * D, D)], ALU.add).then_inc(down_read, 1)
            dve.wait_ge(down_read, s + 1)
            dve.scalar_tensor_tensor(result[:, p, :], result[:, p, :], gates[:, bass.ds(s, 1)], rows[:, k % RING, :],
                                     ALU.mult, ALU.add).then_inc(norm_step, 1)
            dve.wait_ge(norm_step, s * NORM + 1)
            dve.bn_stats(stats[:, p, :], result[:, p, :]).then_inc(norm_step, 1)
            dve.wait_ge(norm_step, s * NORM + 2)
            dve.sem_inc(dve_passed, 1)
            dve.bn_aggr(mv[:, p, :], stats[:, p, :]).then_inc(norm_step, 1)
            dve.wait_ge(norm_step, s * NORM + 3)
            dve.tensor_scalar(centred[:, p, :], result[:, p, :], mv[:, p, 0:1], None,
                              ALU.subtract).then_inc(norm_step, 1)

        def body(s, k):
            dve.wait_ge(up_full, s + 1)
            if not (isinstance(s, int) and s < 2):
                dve.wait_ge(upT_full, s - 1)
            dve.tensor_copy(inner[:, k % 2, :], up[:, :]).then_inc(inner_ready, 1)
            if not (isinstance(s, int) and s == 0):
                residual(s - 1, k - 1)

        steps(dve, body)
        residual(SLOTS - 1, SLOTS - 1)

    @block.tensor
    def _(pe):
        def turn(s, k):
            pe.wait_ge(gathered[k % RING], (s - k % RING) * (16 // RING) + 16)
            if not (isinstance(s, int) and s == 0):
                pe.wait_ge(rowsT_ready, s)
            for c in range(KD):
                last = pe.transpose(turned[:, c * P:(c + 1) * P], rows[:, k % RING, c * P:(c + 1) * P], ident[:, :])
            last.then_inc(turned_full, 1)

        def second(s, k):
            e = expert(pe, s)
            pe.wait_ge(active_ready, s * IC + IC)
            if not (isinstance(s, int) and s < 2):
                pe.wait_ge(down_read, s - 1)
            for c in range(IC):
                last = pe.matmul(down[k % 2][:, :], active[:, k % 2, c, :], w2[:, bass.ds(e, 1), c, :].rearrange(
                    "p o d -> p (o d)"), start=(c == 0), stop=(c == IC - 1))
            last.then_inc(down_full, 1)

        def body(s, k):
            e = expert(pe, s)
            pe.wait_ge(w_seq, e + 1)
            pe.wait_ge(rowsT_ready, s + 1)
            if not (isinstance(s, int) and s == 0):
                pe.wait_ge(inner_ready, s)
            for h in range(I // 512):
                for c in range(KD):
                    last = pe.matmul(up[:, h * 512:(h + 1) * 512], rowsT[:, k % 2, c, :],
                                     w1[:, bass.ds(e, 1), c, h * 512:(h + 1) * 512].rearrange("p o d -> p (o d)"),
                                     start=(c == 0), stop=(c == KD - 1))
            last.then_inc(up_full, 1)
            if not (isinstance(s, int) and s == SLOTS - 1):
                turn(s + 1, k + 1)
            if not (isinstance(s, int) and s == 0):
                second(s - 1, k - 1)
            pe.wait_ge(inner_ready, s + 1)
            if not (isinstance(s, int) and s == 0):
                pe.wait_ge(active_ready, s * IC)
            for c in range(IC):
                last = pe.transpose(upT[:, c * P:(c + 1) * P], inner[:, k % 2, c * P:(c + 1) * P], ident[:, :])
            last.then_inc(upT_full, 1)

        turn(0, 0)
        steps(pe, body)
        second(SLOTS - 1, SLOTS - 1)


_OUT = (B, N, D)


def kernel(**inputs):
    import numpy as _np
    import concourse.bacc as _bacc
    from concourse.bass_utils import run_bass_kernel_spmd as _run

    a = {k: _np.asarray(v) for k, v in inputs.items()}
    x = a["L0_attn_x"]

    def by_row(w):
        return w.T.reshape(KD, P, w.shape[0]).transpose(1, 0, 2)

    wqk = _np.stack([by_row(a[n]) for n in ("L0_attn_Wq", "L0_attn_Wk", "L0_attn_Wk_enc")], 1).reshape(P, 3, KD * D)
    wv = _np.stack([by_row(a[n]) for n in ("L0_attn_Wv", "L0_attn_Wv_enc")], 1).reshape(P, 2 * KD, I)
    arrays = {
        "xT": x.transpose(0, 2, 1).reshape(B, KD, P, N).transpose(0, 2, 1, 3),
        "x": x.reshape(B, NT, P, D).transpose(0, 2, 1, 3),
        "wqk": wqk,
        "wv": wv,
        "wo": a["L0_attn_Wout"].T.reshape(PAIRS, P, D).transpose(1, 0, 2),
        "w1": a["L0_ffn_w1"].reshape(E, KD, P, I).transpose(2, 0, 1, 3),
        "b1": a["L0_ffn_b1"].reshape(E * IC, P).T,
        "w2": a["L0_ffn_w2"].reshape(E, IC, P, D).transpose(2, 0, 1, 3),
        "b2": a["L0_ffn_b2"].reshape(E * D),
        "wr": a["L0_ffn_wr"].reshape(KD, P, E).transpose(1, 0, 2),
        "br": a["L0_ffn_br"],
    }
    arrays = {f"in_{k}": _np.ascontiguousarray(v) for k, v in arrays.items()}
    nc = _bacc.Bacc("TRN2", target_bir_lowering=False, num_devices=1)
    args = [nc.dram_tensor(k, v.shape, mybir.dt.from_np(v.dtype), kind="ExternalInput").ap() for k, v in arrays.items()]
    out = nc.dram_tensor("out", _OUT, F32, kind="ExternalOutput").ap()
    attention_and_experts(nc, *args, out.rearrange("b n d -> (b n) d"))
    r = _run(nc, [arrays], core_ids=[0])
    return r.results[0]["out"]
```

```python
from contextlib import ExitStack

import numpy as np

import concourse.bass as bass
from concourse import mybir

F32 = mybir.dt.float32
F32R = mybir.dt.float32r
BF16 = mybir.dt.bfloat16
I32 = mybir.dt.int32
ALU = mybir.AluOpType
ACT = mybir.ActivationFunctionType
AX = mybir.AxisListType

P = 128
B, N, D = 8, 512, 256
H, FD, HD = 16, 16, 64
NT = N // P
KD = D // P
PAIRS = H // 2
PM = 4
NK = N + P
E, I = 8, 1024
TOK = B * N
TT = TOK // P
IC = I // P
SLOTS = TT + E - 1
CQ = float(1.0 / (4.0 * np.sqrt(2.0)))
HALF_ROOT = float(np.sqrt(0.5))
EPS_Z, EPS_LN = 1e-12, 1e-5
SKIP = 2 * TOK

BLOCKS = [(NT, 0, 0), (0, 0, 512), (1, 128, 1024), (3, 384, 1408), (2, 256, 1536)]
HALVES = [(0, 1024), (1024, 1792)]
XP = 8
ONES = 32
GROUPS = PAIRS // 2
ATT = 4
X_HEADS = (7, 8, 9, 10, 11, 12, 13, 15)
INVERTS = 4
INVERT_AT = {(5, 0): (0, 1), (6, 0): (2, 3)}
SPREAD_AT = {(0, "copied"): (0,), (0, "square0"): (1,), (0, "square1"): (2,), (1, "square0"): (3,), (1, "square1"): (4,)}
RING = 2
U_Q, U_K, U_KE, U_V, U_HEAD = 0, 1, 2, 3, 8
USES = U_HEAD + 2 * H


def attention_and_experts(nc, xT_in, x_in, wqk_in, wv_in, wo_in, w1_in, b1_in, w2_in, b2_in, wr_in, br_in, out):
    ybuf = nc.dram_tensor("attention_rows", [TOK + 1, D], F32).ap()
    with ExitStack() as ctx:
        def sem(name):
            return ctx.enter_context(nc.semaphore(name))

        logits = ctx.enter_context(nc.sbuf_tensor("logits", [P, TT, E], F32))
        ident = ctx.enter_context(nc.sbuf_tensor("ident", [P, P], F32))
        tables = (
            ctx.enter_context(nc.sbuf_tensor("falling", [P, E], F32)),
            ctx.enter_context(nc.sbuf_tensor("tile_starts", [P, TT], F32)),
            ctx.enter_context(nc.sbuf_tensor("count128", [P, P], F32)),
            ctx.enter_context(nc.sbuf_tensor("before", [P, P], BF16)),
            ctx.enter_context(nc.sbuf_tensor("ones", [P, P], BF16)),
            ctx.enter_context(nc.sbuf_tensor("ones32", [P, TT], F32)),
        )
        attention(nc, sem, xT_in, x_in, wqk_in, wv_in, wo_in, wr_in, br_in, ybuf, logits, ident, tables)
        experts(nc, sem, w1_in, b1_in, w2_in, b2_in, ybuf, logits, ident, tables, out)


def attention(nc, sem, xT_in, x_in, wqk_in, wv_in, wo_in, wr_in, br_in, ybuf, logits, ident, tables):
    falling, tile_starts, count128, before, ones, ones32 = tables
    with ExitStack() as ctx:
        def sb(name, shape, dt=F32):
            return ctx.enter_context(nc.sbuf_tensor(name, shape, dt))

        def ps(name, shape):
            return ctx.enter_context(nc.psum_tensor(name, shape, F32))

        wqk_h, wqk_l = sb("wqk_h", [P, 3, KD, D], F32R), sb("wqk_l", [P, 3, KD, D], F32R)
        wv_h, wv_l = sb("wv_h", [P, 2, KD, I], F32R), sb("wv_l", [P, 2, KD, I], F32R)
        wo = sb("wo", [P, PAIRS, D])
        wr = sb("wr", [P, KD, E])
        br = sb("br", [P, E])
        xh, xl = sb("xh", [P, KD, N], F32R), sb("xl", [P, KD, N], F32R)
        qh, ql = sb("qh", [P, 2, N], F32R), sb("ql", [P, 2, N], F32R)
        kh, kl = sb("kh", [P, 2, NK], F32R), sb("kl", [P, 2, NK], F32R)
        qop = sb("qop", [P, RING, 2, N], F32R)
        kop = sb("kop", [P, RING, NK], F32R)
        raw = sb("raw", [P, 2, 1792])
        weights_h, weights_l = sb("weights_h", [P, 2, 1792], F32R), sb("weights_l", [P, 2, 1792], F32R)
        values_h = sb("values_h", [P, NT + 1, H, HD + ONES], F32R)
        values_l = sb("values_l", [P, NT + 1, H, HD], F32R)
        att = sb("att", [P, ATT, N])
        denoms = sb("denoms", [P, 2, N])
        inverse = sb("inverse", [P, N])
        y = sb("y", [P, NT, D])
        xT = y[:, :, :].rearrange("p t d -> p (t d)").rearrange("p (k n) -> p k n", k=KD)
        xrow = raw[:, 1, 0:1024].rearrange("p (t d) -> p t d", t=NT)
        yT = att[:, 0:2, :].rearrange("p b n -> p (b n)").rearrange("p (t n) -> p t n", n=P)
        stats = sb("stats", [P, NT, 6])
        mv = sb("mv", [P, NT, 2])
        eps, minus_half = sb("y_eps", [P, 1]), sb("y_minus_half", [P, 1])
        rstd = sb("rstd", [P, NT])
        zrow = denoms[0:1, 0, 0:D]

        slot = [ps("slot0", [P, 1024]), ps("slot1", [P, 1024])]
        osum = [ps("osum0", [P, N]), ps("osum1", [P, N])]
        ysum = ps("ysum", [P, NT * D])

        w_loaded = [sem("w_loaded0"), sem("w_loaded1")]
        small_loaded = sem("small_loaded")
        w_split = sem("w_split")
        consts = sem("consts")
        zeroed = sem("zeroed")
        filled = sem("filled")
        router_made = sem("router_tables")
        xT_loaded, xrow_loaded = sem("xT_loaded"), sem("xrow_loaded")
        x_split, x_first = sem("x_split"), sem("x_first")
        slot_full = sem("slot_full")
        slot_free = [sem("slot_free0"), sem("slot_free1")]
        qk_hi, qk_lo = sem("qk_hi"), sem("qk_lo")
        op_ready = [sem(f"op_ready{i}") for i in range(RING)]
        odd_ready = [sem(f"odd_ready{i}") for i in range(RING)]
        v_hi = sem("v_hi")
        squared, masked, parts = sem("squared"), sem("masked"), sem("parts")
        w_hi = [sem("w_hi0"), sem("w_hi1")]
        half_used = sem("half_used")
        o_full, copied, divided, att_used = sem("o_full"), sem("copied"), sem("divided"), sem("att_used")
        inverted = sem("inverted")
        spread, moved = sem("spread"), sem("moved")
        y_step, rstd_step, y_ready = sem("y_step"), sem("rstd_step"), sem("y_ready")
        turned, yT_ready = sem("turned"), sem("yT_ready")
        logits_full, logits_read = sem("logits_full"), sem("logits_read")
        y_stored = sem("y_stored")
        pool_passed, dve_passed, sp_passed = sem("pool_passed"), sem("dve_passed"), sem("sp_passed")

        CHUNKS = [(0, 0), (0, 1), (0, 2), (1, 0), (1, 1), (1, 2), (1, 3)]
        STEPS = 1 + 2 * NT
        FREED = U_HEAD // 2

        def use(it, u):
            return it * USES + u

        def batches(eng, body):
            body(0, True, False)
            with eng.Fori(1, B - 1) as it:
                body(it, False, False)
            body(B - 1, False, True)

        block = ctx.enter_context(nc.Block())

        @block.sync
        def _(sp):
            sp.dma_start(xT[:, :, :], xT_in[0]).then_inc(xT_loaded, 16)
            for n, (kind, c) in enumerate(CHUNKS):
                if n >= 2:
                    sp.wait_ge(w_split, 2 * (n - 1))
                src = wqk_in[:, c, :] if kind == 0 else wv_in[:, c, :]
                sp.dma_start(raw[:, n % 2, 0:src.shape[1]], src).then_inc(w_loaded[n % 2], 16)
            sp.dma_start(wo[:, :, :], wo_in).then_inc(small_loaded, 16)
            sp.dma_start(wr[:, :, :], wr_in).then_inc(small_loaded, 16)
            sp.dma_start(br[:, :], br_in.partition_broadcast(P)).then_inc(small_loaded, 16)
            sp.wait_ge(zeroed, 2)
            sp.dma_start(ybuf[0:1, :], zrow).then_inc(small_loaded, 16)

            def body(it, first, last):
                sp.wait_ge(qk_hi, it * 3 + 3)
                sp.wait_ge(qk_lo, it * 3 + 3)
                for p in range(PAIRS):
                    m, r = p // PM, 32 * (p % PM)

                    def used(head):
                        if p >= RING:
                            sp.wait_ge(slot_full, use(it, U_HEAD + 4 * (p - RING) + 2 * head + 2))
                        elif not first:
                            sp.wait_ge(slot_full, use(it, U_HEAD + 4 * (p - RING + PAIRS) + 2 * head + 2) - USES)

                    def queries(s, ready):
                        for c in range(4):
                            i = 32 * c + FD * s
                            sp.dma_start(qop[i:i + FD, p % RING, s, :].bitcast(F32),
                                         (qh, ql, ql, qh)[c][r + FD * s:r + FD * s + FD, m, :].bitcast(F32))\
                                .then_inc(ready[p % RING], 16)

                    used(0)
                    queries(0, op_ready)
                    used(1)
                    for c in range(4):
                        sp.dma_start(kop[32 * c:32 * c + 32, p % RING, :].bitcast(F32),
                                     (kh, kl, kh, kl)[c][r:r + 32, m, :].bitcast(F32)).then_inc(op_ready[p % RING], 16)
                    queries(1, odd_ready)
                    if p == 2 and not first:
                        store(it - 1)
                    if p == 3 and not last:
                        if not first:
                            sp.wait_ge(y_stored, it * 16)
                            sp.sem_inc(sp_passed, 1)
                            sp.wait_ge(turned, it)
                        sp.dma_start(xT[:, :, :], xT_in[it + 1]).then_inc(xT_loaded, 16)

                sp.wait_ge(parts, it * (2 * H) + 2 * H)
                sp.dma_start(xrow[:, :, :], x_in[it]).then_inc(xrow_loaded, 16)

            def store(it):
                sp.wait_ge(y_ready, it * NT + NT)
                sp.dma_start(ybuf[1:TOK + 1, :].rearrange("(b t p) d -> b p t d", p=P, t=NT)[it],
                             y[:, :, :]).then_inc(y_stored, 16)

            batches(sp, body)
            store(B - 1)
            sp.wait_ge(y_stored, 16 * B)
            sp.wait_ge(small_loaded, 64)

        @block.gpsimd
        def _(pool):
            pool.memset(zrow, 0.0).then_inc(zeroed, 1)
            pool.memset(qop[:, :, :, :].bitcast(F32), 0.0).then_inc(zeroed, 1)
            pool.memset(ident[:, :], 0.0).then_inc(filled, 1)
            pool.memset(values_h[:, :, :, HD:HD + ONES].bitcast(F32), 1.0).then_inc(consts, 1)
            pool.memset(eps[:, :], EPS_LN).then_inc(filled, 1)
            pool.memset(minus_half[:, :], -0.5).then_inc(filled, 1)
            pool.wait_ge(filled, 3)
            pool.affine_select(out=ident[:, :], in_=ident[:, :], compare_op=ALU.not_equal, fill=1.0, base=0,
                               pattern=[[-1, P]], channel_multiplier=1).then_inc(consts, 1)

            pool.iota(falling[:, :], [[-1, E]], base=E, channel_multiplier=0,
                      allow_small_or_imprecise_dtypes=True).then_inc(router_made, 1)
            pool.iota(tile_starts[:, :], [[P, TT]], base=0, channel_multiplier=0,
                      allow_small_or_imprecise_dtypes=True).then_inc(router_made, 1)
            pool.iota(count128[:, :], [[1, P]], base=0, channel_multiplier=0,
                      allow_small_or_imprecise_dtypes=True).then_inc(router_made, 1)
            pool.memset(ones32[:, :], 1.0).then_inc(router_made, 1)
            pool.memset(ones[:, :], 1.0).then_inc(router_made, 1)
            pool.memset(before[:, :], 1.0).then_inc(router_made, 1)
            pool.wait_ge(router_made, 6)
            pool.affine_select(out=before[:, :], in_=before[:, :], compare_op=ALU.is_gt, fill=0.0, base=0,
                               pattern=[[1, P]], channel_multiplier=-1).then_inc(router_made, 1)

            def split_x(b, n):
                if n == 0:
                    pool.wait_ge(xT_loaded, b * 16 + 16)
                    pool.sem_inc(pool_passed, 1)
                    pool.wait_ge(slot_full, use(b, U_HEAD) - USES)
                    pool.sem_inc(pool_passed, 1)
                k, c = n * KD // XP, n % (XP // KD) * (KD * N // XP)
                cols = slice(c, c + KD * N // XP)
                pool.tensor_copy(xh[:, k, cols], xT[:, k, cols]).then_inc(x_split, 1)
                pool.wait_ge(x_split, b * (2 * XP) + (2 * n + 1))
                pool.tensor_tensor(xl[:, k, cols], xT[:, k, cols], xh[:, k, cols].bitcast(F32),
                                   ALU.subtract).then_inc(x_split, 1)

            pool.wait_ge(x_first, 1)
            pool.tensor_tensor(xl[:, :, :], xT[:, :, :], xh[:, :, :].bitcast(F32), ALU.subtract).then_inc(x_split, 2 * XP)

            def deviation(b):
                pool.wait_ge(y_step, b * STEPS + STEPS)
                pool.tensor_tensor(rstd[:, :], mv[:, :, 1], eps[:, :].to_broadcast([P, NT]),
                                   ALU.add).then_inc(rstd_step, 1)
                pool.wait_ge(rstd_step, b * 2 + 1)
                pool.tensor_tensor(rstd[:, :], rstd[:, :], minus_half[:, :].to_broadcast([P, NT]),
                                   ALU.pow).then_inc(rstd_step, 1)

            def body(it, first, last):
                def cut(k, a, blocks):
                    w = raw[:, k, a:a + blocks * P].rearrange("p (b c) -> p b c", b=blocks)
                    pool.affine_select(out=w, in_=w, compare_op=ALU.is_ge, fill=-0.5, base=0,
                                       pattern=[[0, blocks], [1, P]], channel_multiplier=-1).then_inc(masked, 1)

                def divide(p):
                    g = p // 2
                    if p % 2 == 0:
                        pool.wait_ge(spread, it * (3 * GROUPS) + (3 * g + 3))
                        by = inverse[:, :]
                    else:
                        by = denoms[:, g % 2, :]
                        pool.wait_ge(moved, it * (2 * GROUPS) + (2 * g + 2))
                    pool.tensor_tensor(att[:, p % ATT, :], att[:, p % ATT, :], by, ALU.mult).then_inc(divided, 1)

                if not first:
                    deviation(it - 1)
                for h in range(H):
                    pool.wait_ge(squared, it * (2 * H) + (2 * h + 1))
                    pool.sem_inc(pool_passed, 1)
                    cut(h % 2, 512, 1)
                    if h in (9, 13):
                        divide((h - 9) // 2)
                    if h in (10, 14):
                        divide((h - 8) // 2)
                    pool.wait_ge(squared, it * (2 * H) + (2 * h + 2))
                    pool.sem_inc(pool_passed, 1)
                    cut(h % 2, 1024, 1)
                    cut(h % 2, 1408, 2)
                    for n in range(XP):
                        if X_HEADS[n] == h and not last:
                            split_x(it + 1, n)
                divide(PAIRS - 4)
                divide(PAIRS - 3)
                divide(PAIRS - 2)
                divide(PAIRS - 1)

            batches(pool, body)
            deviation(B - 1)

        @block.scalar
        def _(act):
            def body(it, first, last):
                def square(h, half):
                    a, b = HALVES[half]
                    u = U_HEAD + 2 * h + half
                    act.wait_ge(slot_full, use(it, u) + 1)
                    if h >= 2 or not first:
                        act.wait_ge(parts, it * (2 * H) + (2 * h - 3 + half))
                    act.activation(raw[:, h % 2, a:b], slot[half][:, 0:b - a], ACT.Square,
                                   bias=HALF_ROOT).then_inc(squared, 1)

                def high_weights(h):
                    a, b = HALVES[1]
                    act.wait_ge(masked, it * (3 * H) + (3 * h + 3))
                    if h >= 2 or not first:
                        act.wait_ge(o_full, it * H + (h - 1))
                    act.activation(weights_h[:, h % 2, a:b], raw[:, h % 2, a:b], ACT.Identity,
                                   bias=0.5).then_inc(w_hi[1], 1)

                def copy_sums(h):
                    p, g, r = h // 2, h // 4, HD * (h % 2)
                    act.wait_ge(o_full, it * H + (h + 1))
                    if p >= ATT or not first:
                        act.wait_ge(att_used, it * PAIRS + (p - ATT + 1))
                    act.activation(att[r:r + HD, p % ATT, :], osum[h % 2][0:HD, :], ACT.Copy).then_inc(copied, 1)
                    if g >= 2 or not first:
                        act.wait_ge(divided, it * PAIRS + (2 * g - 2))
                    r += ONES * (p % 2)
                    act.activation(denoms[r:r + ONES, g % 2, :], osum[h % 2][HD:HD + ONES, :],
                                   ACT.Identity, bias=EPS_Z).then_inc(copied, 1)

                act.wait_ge(slot_full, use(it, U_Q) + 1)
                act.activation(qh[:, :, :], slot[0][:, :].rearrange("p (m n) -> p m n", m=2), ACT.Copy,
                               scale=CQ).then_inc(qk_hi, 1)
                act.wait_ge(slot_full, use(it, U_K) + 1)
                act.activation(kh[:, :, 0:N], slot[1][:, :].rearrange("p (m n) -> p m n", m=2),
                               ACT.Copy).then_inc(qk_hi, 1)
                act.wait_ge(slot_full, use(it, U_KE) + 1)
                act.activation(kh[:, :, N:NK], slot[0][:, 0:2 * P].rearrange("p (m n) -> p m n", m=2),
                               ACT.Copy).then_inc(qk_hi, 1)
                for t in range(NT + 1):
                    if t == 1 and not first:
                        for step in range(5):
                            spread_inverses(it - 1, GROUPS - 1, step)
                    act.wait_ge(slot_full, use(it, U_V + t) + 1)
                    if t == 0 and not first:
                        act.wait_ge(o_full, it * H)
                    act.activation(values_h[:, t, :, 0:HD],
                                   slot[(U_V + t) % 2][:, :].rearrange("p (h d) -> p h d", h=H),
                                   ACT.Copy).then_inc(v_hi, 1)
                def steps(h, behind):
                    if h >= 8:
                        for step in SPREAD_AT.get((h % 4, behind), ()):
                            spread_inverses(it, (h - 8) // 4, step)

                for h in range(H):
                    if h >= 3:
                        copy_sums(h - 3)
                    steps(h, "copied")
                    square(h, 0)
                    steps(h, "square0")
                    if h >= 1:
                        high_weights(h - 1)
                    steps(h, "high")
                    square(h, 1)
                    steps(h, "square1")
                rest = iter(range(5))
                for work in (lambda: copy_sums(H - 3), lambda: high_weights(H - 1), lambda: copy_sums(H - 2),
                             lambda: copy_sums(H - 1)):
                    work()
                    spread_inverses(it, GROUPS - 2, next(rest))
                spread_inverses(it, GROUPS - 2, next(rest))

            def spread_inverses(b, g, step):
                src = denoms[:, g % 2, :]
                r = HD * ((step + 1) % 2)
                if step == 0:
                    act.wait_ge(inverted, b * (INVERTS * GROUPS) + INVERTS * (g + 1))
                    if g > 0 or not (isinstance(b, int) and b == 0):
                        act.wait_ge(divided, b * PAIRS + (2 * g - 1))
                    act.activation(inverse[:, :], src, ACT.Copy).then_inc(spread, 1)
                elif step <= 2:
                    act.wait_ge(spread, b * (3 * GROUPS) + (3 * g + 1))
                    act.activation(inverse[r + ONES:r + HD, :], src[r:r + ONES, :], ACT.Copy).then_inc(spread, 1)
                else:
                    act.wait_ge(spread, b * (3 * GROUPS) + (3 * g + 3))
                    act.activation(src[HD - r:HD - r + ONES, :], src[HD - r + ONES:2 * HD - r, :],
                                   ACT.Copy).then_inc(moved, 1)

            act.wait_ge(xT_loaded, 16)
            act.activation(xh[:, :, :], xT[:, :, :], ACT.Copy).then_inc(x_first, 1)
            batches(act, body)
            for step in range(5):
                spread_inverses(B - 1, GROUPS - 1, step)

        @block.vector
        def _(dve):
            def split_chunk(n):
                kind, c = CHUNKS[n]
                hi, lo = (wqk_h, wqk_l) if kind == 0 else (wv_h, wv_l)
                if kind == 0:
                    hi, lo = hi[:, c, :, :].rearrange("p k n -> p (k n)"), lo[:, c, :, :].rearrange("p k n -> p (k n)")
                else:
                    hi, lo = hi[:, c // 2, c % 2, :], lo[:, c // 2, c % 2, :]
                src = raw[:, n % 2, 0:hi.shape[1]]
                dve.wait_ge(w_loaded[n % 2], 16 * (n // 2 + 1))
                dve.tensor_copy(hi, src).then_inc(w_split, 1)
                dve.wait_ge(w_split, 2 * n + 1)
                dve.tensor_tensor(lo, src, hi.bitcast(F32), ALU.subtract).then_inc(w_split, 1)

            for n in range(5):
                split_chunk(n)

            def body(it, first, last):
                def low(dst, src, factor, hi, n, free):
                    dve.wait_ge(qk_hi, it * 3 + n)
                    dve.scalar_tensor_tensor(dst, src, factor, hi.bitcast(F32), ALU.mult, ALU.subtract).then_inc(qk_lo, 1)
                    dve.wait_ge(qk_lo, it * 3 + n)
                    dve.sem_inc(slot_free[free], 1)

                def low_values(t):
                    dve.wait_ge(v_hi, it * (NT + 1) + (t + 1))
                    u = U_V + t
                    dve.tensor_tensor(values_l[:, t, :, :], slot[u % 2][:, :].rearrange("p (h d) -> p h d", h=H),
                                      values_h[:, t, :, 0:HD].bitcast(F32), ALU.subtract).then_inc(slot_free[u % 2], 1)

                def split_weights(h, k):
                    a, b = HALVES[k]
                    src = raw[:, h % 2, a:b]
                    if k == 0:
                        dve.wait_ge(masked, it * (3 * H) + (3 * h + 1))
                        if h >= 2 or not first:
                            dve.wait_ge(half_used, it * H + (h - 1))
                        dve.tensor_scalar(weights_h[:, h % 2, a:b], src, 0.5, None, ALU.add).then_inc(w_hi[0], 1)
                    dve.wait_ge(w_hi[k], it * H + (h + 1))
                    dve.scalar_tensor_tensor(weights_l[:, h % 2, a:b], src, 0.5,
                                             weights_h[:, h % 2, a:b].bitcast(F32), ALU.add,
                                             ALU.subtract).then_inc(parts, 1)

                m2 = "p (m n) -> p m n"
                low(ql[:, :, :], slot[0][:, :].rearrange(m2, m=2), CQ, qh[:, :, :], 1, 0)
                low(kl[:, :, 0:N], slot[1][:, :].rearrange(m2, m=2), 1.0, kh[:, :, 0:N], 2, 1)
                low(kl[:, :, N:NK], slot[0][:, 0:2 * P].rearrange(m2, m=2), 1.0, kh[:, :, N:NK], 3, 0)
                if first:
                    split_chunk(5)
                    split_chunk(6)
                if not first:
                    for k in range(INVERTS):
                        invert(it - 1, GROUPS - 1, k)
                low_values(0)
                low_values(1)
                low_values(2)
                if not first:
                    residual(it - 1)
                    moments(it - 1)
                low_values(3)
                if not first:
                    normalise(it - 1)
                low_values(4)
                if not first:
                    turned_rows(it - 1)

                def inverts(h, half):
                    if h >= 5:
                        for k in INVERT_AT.get(((h - 5) % 4 + 5, half), ()):
                            invert(it, (h - 5) // 4, k)

                for h in range(H):
                    split_weights(h, 0)
                    if h == 0 and not first:
                        logits_of(it - 1)
                    inverts(h, 0)
                    split_weights(h, 1)
                    inverts(h, 1)

            def invert(b, g, k):
                dve.wait_ge(copied, b * (2 * H) + (8 * g + 8))
                part = denoms[:, g % 2, k * N // INVERTS:(k + 1) * N // INVERTS]
                dve.reciprocal(part, part).then_inc(inverted, 1)

            def residual(b):
                dve.wait_ge(att_used, b * PAIRS + PAIRS)
                dve.wait_ge(xrow_loaded, b * 16 + 16)
                if not (isinstance(b, int) and b == 0):
                    dve.wait_ge(y_stored, b * 16)
                dve.tensor_tensor(y[:, :, :], ysum[:, :].rearrange("p (t d) -> p t d", t=NT), xrow[:, :, :],
                                  ALU.add).then_inc(y_step, 1)

            def moments(b):
                dve.wait_ge(y_step, b * STEPS + 1)
                for t in range(NT):
                    dve.bn_stats(stats[:, t, :], y[:, t, :]).then_inc(y_step, 1)
                dve.wait_ge(y_step, b * STEPS + (1 + NT))
                dve.sem_inc(dve_passed, 1)
                for t in range(NT):
                    dve.bn_aggr(mv[:, t, :], stats[:, t, :]).then_inc(y_step, 1)

            def normalise(b):
                dve.wait_ge(rstd_step, b * 2 + 2)
                for t in range(NT):
                    dve.tensor_scalar(y[:, t, :], y[:, t, :], mv[:, t, 0:1], rstd[:, t:t + 1], ALU.subtract,
                                      ALU.mult).then_inc(y_ready, 1)

            def turned_rows(b):
                dve.wait_ge(turned, b + 1)
                for k in range(2):
                    dve.tensor_copy(yT[:, 4 * k:4 * k + 4, :],
                                    osum[k][:, :].rearrange("p (t n) -> p t n", n=P)).then_inc(yT_ready, 1)

            def logits_of(b):
                dve.wait_ge(logits_full, b + 1)
                dve.tensor_tensor(logits[:, bass.ts(b, NT), :], osum[1][:, 0:NT * E].rearrange("p (t e) -> p t e", e=E),
                                  br[:, :].unsqueeze(1).to_broadcast([P, NT, E]), ALU.add).then_inc(logits_read, 1)

            batches(dve, body)
            for k in range(INVERTS):
                invert(B - 1, GROUPS - 1, k)
            residual(B - 1)
            moments(B - 1)
            normalise(B - 1)
            turned_rows(B - 1)
            logits_of(B - 1)

        @block.tensor
        def _(pe):
            def three(dst, wh, wl, vh, vl):
                parts = [(wh, vh), (wh, vl), (wl, vh)]
                for n, (a, b) in enumerate((a, b) for a in range(3) for b in range(KD)):
                    last = pe.matmul(dst, parts[a][0](b), parts[a][1](b), start=(n == 0), stop=(n == 3 * KD - 1))
                return last

            def take(it, u):
                if u >= 2:
                    pe.wait_ge(slot_free[u % 2], it * FREED + u // 2)
                elif not (isinstance(it, int) and it == 0):
                    pe.wait_ge(squared, it * (2 * H))

            def turn_rows(b):
                pe.wait_ge(y_ready, b * NT + NT)
                pe.wait_ge(copied, b * (2 * H) + 2 * H)
                for t in range(NT):
                    for k in range(KD):
                        n = t * KD + k
                        last = pe.transpose(osum[n // 4][:, n % 4 * P:n % 4 * P + P], y[:, t, k * P:(k + 1) * P],
                                            ident[:, :])
                last.then_inc(turned, 1)

            def router(b):
                pe.wait_ge(yT_ready, b * 2 + 2)
                for t in range(NT):
                    for k in range(KD):
                        last = pe.matmul(osum[1][:, t * E:(t + 1) * E], yT[:, t * KD + k, :], wr[:, k, :],
                                         start=(k == 0), stop=(k == KD - 1))
                last.then_inc(logits_full, 1)

            def output(it, p):
                pe.wait_ge(divided, it * PAIRS + (p + 1))
                if p == 0 and not (isinstance(it, int) and it == 0):
                    pe.wait_ge(y_step, it * STEPS - (STEPS - 1))
                for t in range(NT):
                    last = pe.matmul(ysum[:, t * D:(t + 1) * D], att[:, p % ATT, t * P:(t + 1) * P], wo[:, p, :],
                                     start=(p == 0 and t % 2 == 0), stop=(p == PAIRS - 1), skip_group_check=True)
                    if t == NT - 1:
                        last.then_inc(att_used, 1)

            def body(it, first, last_batch):
                def project_qk(u, w, cols, sl):
                    take(it, u)
                    for m in range(2):
                        lo, hi = m * P, (m + 1) * P
                        last = three(slot[sl][:, m * cols:(m + 1) * cols],
                                     lambda k: wqk_h[:, w, k, lo:hi], lambda k: wqk_l[:, w, k, lo:hi],
                                     lambda k: xh[:, k, 0:cols], lambda k: xl[:, k, 0:cols])
                    last.then_inc(slot_full, 1)

                def project_values(t):
                    u, enc = U_V + t, int(t == NT)
                    a = 0 if enc else t * P
                    take(it, u)
                    for c in range(2):
                        last = three(slot[u % 2][:, c * 512:(c + 1) * 512],
                                     lambda k: xh[:, k, a:a + P], lambda k: xl[:, k, a:a + P],
                                     lambda k: wv_h[:, enc, k, c * 512:(c + 1) * 512],
                                     lambda k: wv_l[:, enc, k, c * 512:(c + 1) * 512])
                    last.then_inc(slot_full, 1)

                def scores(h, half):
                    p = h // 2
                    if h % 2 == 0 and half == 0:
                        pe.wait_ge(op_ready[p % RING], it * (128 * PAIRS // RING) + 128 * (p // RING + 1))
                    if h % 2 == 1 and half == 0:
                        pe.wait_ge(odd_ready[p % RING], it * (64 * PAIRS // RING) + 64 * (p // RING + 1))
                    if h == 0:
                        pe.wait_ge(slot_free[half], it * FREED + FREED)
                    else:
                        pe.wait_ge(squared, it * (2 * H) + (2 * h + half - 1))
                    off = HALVES[half][0]
                    for j, q0, col in BLOCKS[2 * half:2 * half + 2 + half]:
                        k0 = j * P
                        last = pe.matmul(slot[half][:, col - off:col - off + N - q0], kop[:, p % RING, k0:k0 + P],
                                         qop[:, p % RING, h % 2, q0:N], start=True, stop=True)
                    last.then_inc(slot_full, 1)

                def weigh(h, half):
                    pe.wait_ge(parts, it * (2 * H) + (2 * h + half + 1))
                    if half == 0 and (h >= 2 or not first):
                        pe.wait_ge(copied, it * (2 * H) + (2 * h - 2))
                    if half == 0 and h == 1 and not first:
                        pe.wait_ge(logits_read, it)
                    for n, (j, q0, col) in enumerate(BLOCKS[2 * half:2 * half + 2 + half]):
                        vh = values_h[:, j, h, :]
                        wh, wl = weights_h[:, h % 2, col:col + N - q0], weights_l[:, h % 2, col:col + N - q0]
                        dst = osum[h % 2][0:HD + ONES, :]
                        pe.matmul(dst[:, q0:N], vh, wh, start=(half == 0 and n == 0), stop=False)
                        pe.matmul(dst[0:HD, q0:N], values_l[:, j, h, :], wh, start=False, stop=False)
                        last = pe.matmul(dst[:, q0:N], vh, wl, start=False, stop=(half == 1 and n == 2))
                    last.then_inc((half_used, o_full)[half], 1)

                if first:
                    pe.wait_ge(w_split, 6)
                pe.wait_ge(x_split, it * (2 * XP) + 2 * XP)
                project_qk(U_Q, 0, N, 0)
                project_qk(U_K, 1, N, 1)
                project_qk(U_KE, 2, P, 0)
                if first:
                    pe.wait_ge(w_split, 2 * (len(CHUNKS) - 2))
                    pe.wait_ge(small_loaded, 64)
                    pe.wait_ge(consts, 2)
                if not first:
                    output(it - 1, PAIRS - 4)
                    output(it - 1, PAIRS - 3)
                for t in range(NT + 1):
                    if t == NT and first:
                        pe.wait_ge(w_split, 2 * len(CHUNKS))
                    project_values(t)
                    if t == 2 and not first:
                        last_output(it - 1)
                scores(0, 0)
                if not first:
                    turn_rows(it - 1)
                scores(0, 1)
                scores(1, 0)
                if not first:
                    router(it - 1)
                scores(1, 1)
                for h in range(H):
                    if h + 2 < H:
                        scores(h + 2, 0)
                    weigh(h, 0)
                    if h + 2 < H:
                        scores(h + 2, 1)
                    weigh(h, 1)
                    if h in (8, 9, 12, 13):
                        output(it, {8: 0, 9: 1, 12: 2, 13: 3}[h])

            def last_output(b):
                output(b, PAIRS - 2)
                output(b, PAIRS - 1)

            batches(pe, body)
            output(B - 1, PAIRS - 4)
            output(B - 1, PAIRS - 3)
            last_output(B - 1)
            turn_rows(B - 1)
            router(B - 1)


def experts(nc, sem, w1_in, b1_in, w2_in, b2_in, ybuf, logits, ident, tables, out):
    with ExitStack() as ctx:
        def sb(name, shape, dt=F32):
            return ctx.enter_context(nc.sbuf_tensor(name, shape, dt))

        def ps(name, shape):
            return ctx.enter_context(nc.psum_tensor(name, shape, F32))

        w1 = sb("w1", [P, E, KD, I])
        w2 = sb("w2", [P, E, IC, D])
        b1 = sb("b1", [P, E * IC])
        b2 = sb("b2", [P, E * D])
        row_index = sb("row_index", [P, SLOTS], I32)
        out_index = sb("out_index", [P, SLOTS], I32)
        gates = sb("gates", [P, SLOTS])
        expert_of = sb("expert_of", [P, SLOTS], I32)

        w_seq = sem("expert_weights")
        table_loaded = sem("table_loaded")
        w_sem = [sem("expert_loaded0"), sem("expert_loaded1")]
        routed = sem("routed")

        with ExitStack() as inner:
            route(nc, inner, sem, w_seq, table_loaded, w_sem, routed, w1, w2, b1, b2, w1_in, w2_in, b1_in, b2_in,
                  logits, tables, row_index, out_index, gates, expert_of)
        run_experts(nc, ctx, sem, w_seq, w1, w2, b1, b2, row_index, out_index, gates, expert_of,
                    ybuf, ident, out, w_sem, w1_in, w2_in)


EVEN = SLOTS + SLOTS % 2
CODED = 8
LOADED_EARLY = 2


def load_expert(sp, e, w1, w2, w1_in, w2_in, w_sem):
    sp.dma_start(w1[:, e, :, :], w1_in[:, e, :, :]).then_inc(w_sem[e % 2], 16)
    sp.dma_start(w2[:, e, :, :], w2_in[:, e, :, :]).then_inc(w_sem[e % 2], 16)


def route(nc, ctx, sem, w_seq, table_loaded, w_sem, routed, w1, w2, b1, b2, w1_in, w2_in, b1_in, b2_in,
          logits, tables, row_index, out_index, gates, expert_of):
    falling, tile_starts, count128, before, ones, ones32 = tables

    def sb(name, shape, dt=F32):
        return ctx.enter_context(nc.sbuf_tensor(name, shape, dt))

    def ps(name, shape):
        return ctx.enter_context(nc.psum_tensor(name, shape, F32))

    token1 = sb("token1", [P, TT])
    top = sb("top", [P, TT])
    second = sb("second", [P, TT])
    key = sb("key", [P, TT, E])
    hot = sb("hot", [P, TT, E], BF16)
    rest = sb("rest", [P, TT, E])
    gate = sb("gate", [P, TT])
    gate_h, gate_l = sb("gate_h", [P, TT], F32R), sb("gate_l", [P, TT], F32R)
    kmax = sb("kmax", [P, TT])
    cum = sb("cum", [P, E, TT])
    more = sb("more", [P, E, TT])
    used = sb("used", [P, E])
    last_slot = sb("last_slot", [P, E])
    first_row = sb("first_row", [P, E])
    place = sb("place", [P, TT, E])
    pos = sb("pos", [P, TT])
    pos_i = sb("pos_i", [P, TT], I32)
    slot_i = sb("slot_i", [P, TT], I32)
    row_i = sb("row_i", [P, TT], I32)
    slot_f = sb("slot_f", [P, TT])
    row_f = sb("row_f", [P, TT])
    in_slot = sb("in_slot", [P, TT, EVEN])
    carried = sb("carried", [P, TT, 3, EVEN], F32R)
    in_row = sb("in_row", [P, TT, P], F32R)
    passed = sb("passed", [P, SLOTS, E - 1])
    expert_f = sb("expert_f", [P, SLOTS])
    index_f = sb("index_f", [P, SLOTS])
    empty = sb("empty", [P, SLOTS])
    ranks = ps("ranks", [P, TT * E])
    totals = ps("totals", [P, TT * E])
    found = ps("found", [P, 3 * EVEN])

    made = sem("route_consts")
    step = sem("route_step")
    counted = sem("counted")
    exp_in, exp_out = sem("exp_in"), sem("exp_out")
    placed = sem("placed")
    found_all = sem("found_all")

    block = ctx.enter_context(nc.Block())

    @block.sync
    def _(sp):
        sp.dma_start(b1[:, :], b1_in).then_inc(table_loaded, 16)
        sp.dma_start(b2[:, :], b2_in.partition_broadcast(P)).then_inc(table_loaded, 16)
        for e in range(LOADED_EARLY):
            load_expert(sp, e, w1, w2, w1_in, w2_in, w_sem)
        sp.wait_ge(table_loaded, 32)

    @block.gpsimd
    def _(pool):
        pool.iota(token1[:, :], [[P, TT]], base=1, channel_multiplier=1,
                  allow_small_or_imprecise_dtypes=True).then_inc(made, 1)

    @block.scalar
    def _(act):
        act.wait_ge(exp_in, 1)
        act.activation(gate[:, :], second[:, :], ACT.Exp).then_inc(exp_out, 1)

    @block.tensor
    def _(pe):
        pe.wait_ge(counted, 1)
        flat = hot[:, :, :].rearrange("p t e -> p (t e)")
        pe.matmul(ranks[:, :], before[:, :], flat, start=True, stop=True)
        pe.matmul(totals[:, :], ones[:, :], flat, start=True, stop=True).then_inc(counted, 1)
        for t in range(TT):
            if t % (TT // CODED) == 0:
                pe.wait_ge(placed, t // (TT // CODED) + 1)
            last = pe.matmul(found[:, :], in_row[:, t, :], carried[:, t, :, :].rearrange("p a s -> p (a s)"),
                             start=(t == 0), stop=(t == TT - 1))
        last.then_inc(found_all, 1)

    @block.vector
    def _(dve):
        n = [0]

        def after(op):
            n[0] += 1
            op.then_inc(step, 1)
            dve.wait_ge(step, n[0])

        def over_e(ap):
            return ap.unsqueeze(2).to_broadcast([P, TT, E])

        def over_t(ap):
            return ap.unsqueeze(1).to_broadcast([P, TT, E])

        after(dve.tensor_reduce(top[:, :], logits[:, :, :], AX.X, ALU.max))
        after(dve.tensor_tensor(key[:, :, :], logits[:, :, :], over_e(top[:, :]), ALU.is_ge))
        after(dve.tensor_tensor(key[:, :, :], key[:, :, :], over_t(falling[:, :]), ALU.mult))
        after(dve.tensor_reduce(kmax[:, :], key[:, :, :], AX.X, ALU.max))
        after(dve.tensor_tensor(hot[:, :, :], over_t(falling[:, :]), over_e(kmax[:, :]), ALU.is_equal))
        dve.sem_inc(counted, 1)
        after(dve.scalar_tensor_tensor(rest[:, :, :], hot[:, :, :], -3.0e38, logits[:, :, :], ALU.mult, ALU.add))
        after(dve.tensor_reduce(second[:, :], rest[:, :, :], AX.X, ALU.max))
        after(dve.tensor_tensor(second[:, :], second[:, :], top[:, :], ALU.subtract))
        dve.sem_inc(exp_in, 1)
        dve.wait_ge(counted, 2)
        by_tile = totals[:, :].rearrange("p (t e) -> p t e", e=E)
        for e in range(E):
            op = dve.tensor_tensor_scan(cum[:, e, :], ones32[:, :], by_tile[:, :, e], 0.0, ALU.mult, ALU.add)
            if e < E - 1:
                n[0] += 1
                op.then_inc(step, 1)
        after(op)
        after(dve.tensor_tensor(more[:, :, :], cum[:, :, TT - 1:TT].to_broadcast([P, E, TT]),
                                tile_starts[:, :].unsqueeze(1).to_broadcast([P, E, TT]), ALU.is_gt))
        after(dve.tensor_reduce(used[:, :], more[:, :, :], AX.X, ALU.add))
        after(dve.tensor_scalar(used[:, :], used[:, :], 1.0, None, ALU.max))
        after(dve.tensor_tensor_scan(last_slot[:, :], ones32[:, 0:E], used[:, :], 0.0, ALU.mult, ALU.add))
        after(dve.tensor_tensor(first_row[:, :], last_slot[:, :], used[:, :], ALU.subtract))
        after(dve.tensor_scalar(first_row[:, :], first_row[:, :], float(P), None, ALU.mult))
        after(dve.tensor_tensor(place[:, :, :], cum[:, :, :].rearrange("p e t -> p t e"), by_tile, ALU.subtract))
        after(dve.tensor_tensor(place[:, :, :], place[:, :, :], ranks[:, :].rearrange("p (t e) -> p t e", e=E),
                                ALU.add))
        after(dve.tensor_tensor(place[:, :, :], place[:, :, :], over_t(first_row[:, :]), ALU.add))
        after(dve.tensor_tensor(place[:, :, :], place[:, :, :], hot[:, :, :], ALU.mult))
        after(dve.tensor_reduce(pos[:, :], place[:, :, :], AX.X, ALU.add))
        after(dve.tensor_copy(pos_i[:, :], pos[:, :]))
        after(dve.tensor_scalar(slot_i[:, :], pos_i[:, :], 7, None, ALU.logical_shift_right))
        after(dve.tensor_scalar(row_i[:, :], pos_i[:, :], P - 1, None, ALU.bitwise_and))
        after(dve.tensor_copy(slot_f[:, :], slot_i[:, :]))
        after(dve.tensor_copy(row_f[:, :], row_i[:, :]))
        after(dve.tensor_tensor(in_slot[:, :, :], count128[:, 0:EVEN].unsqueeze(1).to_broadcast([P, TT, EVEN]),
                                slot_f[:, :].unsqueeze(2).to_broadcast([P, TT, EVEN]), ALU.is_equal))
        dve.wait_ge(exp_out, 1)
        after(dve.tensor_scalar(gate[:, :], gate[:, :], 1.0, None, ALU.add))
        after(dve.reciprocal(gate[:, :], gate[:, :]))
        after(dve.tensor_copy(gate_h[:, :], gate[:, :]))
        after(dve.tensor_tensor(gate_l[:, :], gate[:, :], gate_h[:, :].bitcast(F32), ALU.subtract))
        dve.wait_ge(made, 1)
        for k, value in enumerate((token1[:, :], gate_h[:, :].bitcast(F32), gate_l[:, :].bitcast(F32))):
            after(dve.tensor_tensor(carried[:, :, k, :], in_slot[:, :, :],
                                    value.unsqueeze(2).to_broadcast([P, TT, EVEN]), ALU.mult))
        for c in range(CODED):
            n_t = TT // CODED
            tiles = slice(c * n_t, (c + 1) * n_t)
            dve.tensor_tensor(in_row[:, tiles, :], count128[:, :].unsqueeze(1).to_broadcast([P, n_t, P]),
                              row_f[:, tiles].unsqueeze(2).to_broadcast([P, n_t, P]),
                              ALU.is_equal).then_inc(placed, 1)
        after(dve.tensor_tensor(passed[:, :, :], count128[:, 0:SLOTS].unsqueeze(2).to_broadcast([P, SLOTS, E - 1]),
                                last_slot[:, 0:E - 1].unsqueeze(1).to_broadcast([P, SLOTS, E - 1]), ALU.is_ge))
        after(dve.tensor_reduce(expert_f[:, :], passed[:, :, :], AX.X, ALU.add))
        after(dve.tensor_copy(expert_of[:, :], expert_f[:, :]))
        dve.wait_ge(found_all, 1)
        after(dve.tensor_copy(row_index[:, :], found[:, 0:SLOTS]))
        after(dve.tensor_copy(gates[:, :], found[:, EVEN:EVEN + SLOTS]))
        after(dve.tensor_tensor(gates[:, :], gates[:, :], found[:, 2 * EVEN:2 * EVEN + SLOTS], ALU.add))
        after(dve.tensor_scalar(empty[:, :], found[:, 0:SLOTS], 0.0, float(SKIP + 1), ALU.is_equal, ALU.mult))
        after(dve.scalar_tensor_tensor(index_f[:, :], found[:, 0:SLOTS], -1.0, empty[:, :], ALU.add, ALU.add))
        after(dve.tensor_copy(out_index[:, :], index_f[:, :]))
        dve.sem_inc(routed, 1)


def run_experts(nc, ctx, sem, w_seq, w1, w2, b1, b2, row_index, out_index, gates, expert_of,
                ybuf, ident, out, w_sem, w1_in, w2_in):
    RING = 4
    UNROLL = 4
    PEELED = 3

    def sb(name, shape, dt=F32):
        return ctx.enter_context(nc.sbuf_tensor(name, shape, dt))

    def ps(name, shape):
        return ctx.enter_context(nc.psum_tensor(name, shape, F32))

    rows = sb("rows", [P, RING, D])
    rows_col = sb("rows_col", [P, RING], I32)
    out_col = sb("out_col", [P, 2], I32)
    rowsT = sb("rowsT", [P, 2, KD, P])
    inner = sb("inner", [P, 2, I])
    active = sb("active", [P, 2, IC, P])
    result = sb("result", [P, 2, D])
    centred = sb("centred", [P, 2, D])
    final = sb("final", [P, 2, D])
    stats = sb("e_stats", [P, 2, 6])
    mv = sb("e_mv", [P, 2, 2])
    rs = sb("e_rs", [P, 2])
    eps = sb("eps", [P, 1])
    minus_half = sb("minus_half", [P, 1])

    turned = ps("turned", [P, KD * P])
    up = ps("up", [P, I])
    upT = ps("upT", [P, I])
    down = [ps("down0", [P, D]), ps("down1", [P, D])]

    gathered = [sem(f"gathered{i}") for i in range(RING)]
    indexed, ready_consts = sem("indexed"), sem("loop_consts")
    turned_full, rowsT_ready = sem("turned_full"), sem("rowsT_ready")
    up_full, inner_ready = sem("up_full"), sem("inner_ready")
    upT_full, active_ready = sem("upT_full"), sem("active_ready")
    down_full, down_read = sem("down_full"), sem("down_read")
    norm_step, final_step = sem("norm_step"), sem("final_step")
    scattered = [sem("scattered0"), sem("scattered1")]
    passed, dve_passed = sem("loop_passed"), sem("loop_dve_passed")
    NORM = 4
    FINAL = 4

    def steps(eng, body):
        for s in range(PEELED):
            body(s, s)
        loops = (SLOTS - PEELED - 1) // UNROLL
        with eng.Fori(0, loops) as i:
            for j in range(UNROLL):
                body(i * UNROLL + (PEELED + j), PEELED + j)
        for s in range(PEELED + loops * UNROLL, SLOTS):
            body(s, s)

    def expert(eng, s):
        return eng.value_load(expert_of[0:1, bass.ds(s, 1)], min_val=0, max_val=E - 1)

    block = ctx.enter_context(nc.Block())

    @block.sync
    def _(sp):
        for e in range(LOADED_EARLY, E):
            load_expert(sp, e, w1, w2, w1_in, w2_in, w_sem)
            sp.wait_ge(w_sem[(e - 1) % 2], 32 * ((e - 1) // 2 + 1))
            if e - 1 == LOADED_EARLY - 1:
                sp.sem_inc(w_seq, LOADED_EARLY)
            else:
                sp.sem_inc(w_seq, 1)
        sp.wait_ge(w_sem[(E - 1) % 2], 32 * ((E - 1) // 2 + 1))
        sp.sem_inc(w_seq, 1)

    @block.gpsimd
    def _(pool):
        pool.memset(eps[:, :], EPS_LN).then_inc(ready_consts, 1)
        pool.memset(minus_half[:, :], -0.5).then_inc(ready_consts, 1)
        pool.wait_ge(ready_consts, 2)

        def gather(s, k):
            pool.tensor_copy(rows_col[:, k % RING:k % RING + 1], row_index[:, bass.ds(s, 1)]).then_inc(indexed, 1)
            pool.wait_ge(indexed, s + 1)
            pool.sem_inc(passed, 1)
            pool.indirect_dma_start(rows[:, k % RING, :], None, ybuf[:, :],
                                    bass.IndirectOffsetOnAxis(ap=rows_col[:, k % RING:k % RING + 1], axis=0))\
                .then_inc(gathered[k % RING], 16)

        def finish(s, k):
            p = k % 2
            if not (isinstance(s, int) and s < 2):
                pool.wait_ge(scattered[p], (s - p) * 8)
                pool.sem_inc(passed, 1)
            pool.tensor_copy(out_col[:, p:p + 1], out_index[:, bass.ds(s, 1)]).then_inc(final_step, 1)
            pool.wait_ge(norm_step, s * NORM + NORM)
            pool.tensor_tensor(rs[:, p:p + 1], mv[:, p, 1:2], eps[:, :], ALU.add).then_inc(final_step, 1)
            pool.wait_ge(final_step, s * FINAL + 2)
            pool.tensor_tensor(rs[:, p:p + 1], rs[:, p:p + 1], minus_half[:, :], ALU.pow).then_inc(final_step, 1)
            pool.wait_ge(final_step, s * FINAL + 3)
            pool.tensor_tensor(final[:, p, :], centred[:, p, :], rs[:, p:p + 1].to_broadcast([P, D]),
                               ALU.mult).then_inc(final_step, 1)
            pool.wait_ge(final_step, s * FINAL + 4)
            pool.sem_inc(passed, 1)
            pool.indirect_dma_start(out, bass.IndirectOffsetOnAxis(ap=out_col[:, p:p + 1], axis=0), final[:, p, :],
                                    None, bounds_check=TOK - 1, oob_is_err=False).then_inc(scattered[p], 16)

        for s in range(3):
            gather(s, s)
        finish(0, 0)
        gather(3, 3)
        with pool.Fori(0, (SLOTS - 7) // UNROLL) as i:
            for j in range(UNROLL):
                gather(i * UNROLL + (4 + j), 4 + j)
                finish(i * UNROLL + (1 + j), 1 + j)
        for s in range(SLOTS - 6, SLOTS):
            if s + 3 < SLOTS:
                gather(s + 3, s + 3)
            finish(s, s)
        for p in range(2):
            pool.wait_ge(scattered[p], 16 * ((SLOTS + 1 - p) // 2))

    @block.scalar
    def _(act):
        def turn(s, k):
            act.wait_ge(turned_full, s + 1)
            if not (isinstance(s, int) and s < 2):
                act.wait_ge(up_full, s - 1)
            act.activation(rowsT[:, k % 2, :, :], turned[:, :].rearrange("p (k n) -> p k n", k=KD),
                           ACT.Copy).then_inc(rowsT_ready, 1)

        def body(s, k):
            if not (isinstance(s, int) and s == SLOTS - 1):
                turn(s + 1, k + 1)
            e = expert(act, s)
            act.wait_ge(upT_full, s + 1)
            if not (isinstance(s, int) and s < 2):
                act.wait_ge(down_full, s - 1)
            for c in range(IC):
                act.activation(active[:, k % 2, c, :], upT[:, c * P:(c + 1) * P], ACT.Gelu,
                               bias=b1[:, bass.ds(e * IC + c, 1)]).then_inc(active_ready, 1)

        turn(0, 0)
        steps(act, body)

    @block.vector
    def _(dve):
        def residual(s, k):
            p = k % 2
            e = expert(dve, s)
            dve.wait_ge(down_full, s + 1)
            if not (isinstance(s, int) and s < 2):
                dve.wait_ge(final_step, s * FINAL - FINAL)
            dve.tensor_tensor(result[:, p, :], down[p][:, :], b2[:, bass.ds(e * D, D)], ALU.add).then_inc(down_read, 1)
            dve.wait_ge(down_read, s + 1)
            dve.scalar_tensor_tensor(result[:, p, :], result[:, p, :], gates[:, bass.ds(s, 1)], rows[:, k % RING, :],
                                     ALU.mult, ALU.add).then_inc(norm_step, 1)
            dve.wait_ge(norm_step, s * NORM + 1)
            dve.bn_stats(stats[:, p, :], result[:, p, :]).then_inc(norm_step, 1)
            dve.wait_ge(norm_step, s * NORM + 2)
            dve.sem_inc(dve_passed, 1)
            dve.bn_aggr(mv[:, p, :], stats[:, p, :]).then_inc(norm_step, 1)
            dve.wait_ge(norm_step, s * NORM + 3)
            dve.tensor_scalar(centred[:, p, :], result[:, p, :], mv[:, p, 0:1], None,
                              ALU.subtract).then_inc(norm_step, 1)

        def body(s, k):
            dve.wait_ge(up_full, s + 1)
            if not (isinstance(s, int) and s < 2):
                dve.wait_ge(upT_full, s - 1)
            dve.tensor_copy(inner[:, k % 2, :], up[:, :]).then_inc(inner_ready, 1)
            if not (isinstance(s, int) and s == 0):
                residual(s - 1, k - 1)

        steps(dve, body)
        residual(SLOTS - 1, SLOTS - 1)

    @block.tensor
    def _(pe):
        def turn(s, k):
            pe.wait_ge(gathered[k % RING], (s - k % RING) * (16 // RING) + 16)
            if not (isinstance(s, int) and s == 0):
                pe.wait_ge(rowsT_ready, s)
            for c in range(KD):
                last = pe.transpose(turned[:, c * P:(c + 1) * P], rows[:, k % RING, c * P:(c + 1) * P], ident[:, :])
            last.then_inc(turned_full, 1)

        def second(s, k):
            e = expert(pe, s)
            pe.wait_ge(active_ready, s * IC + IC)
            if not (isinstance(s, int) and s < 2):
                pe.wait_ge(down_read, s - 1)
            for c in range(IC):
                last = pe.matmul(down[k % 2][:, :], active[:, k % 2, c, :], w2[:, bass.ds(e, 1), c, :].rearrange(
                    "p o d -> p (o d)"), start=(c == 0), stop=(c == IC - 1))
            last.then_inc(down_full, 1)

        def body(s, k):
            e = expert(pe, s)
            pe.wait_ge(w_seq, e + 1)
            pe.wait_ge(rowsT_ready, s + 1)
            if not (isinstance(s, int) and s == 0):
                pe.wait_ge(inner_ready, s)
            for h in range(I // 512):
                for c in range(KD):
                    last = pe.matmul(up[:, h * 512:(h + 1) * 512], rowsT[:, k % 2, c, :],
                                     w1[:, bass.ds(e, 1), c, h * 512:(h + 1) * 512].rearrange("p o d -> p (o d)"),
                                     start=(c == 0), stop=(c == KD - 1))
            last.then_inc(up_full, 1)
            if not (isinstance(s, int) and s == SLOTS - 1):
                turn(s + 1, k + 1)
            if not (isinstance(s, int) and s == 0):
                second(s - 1, k - 1)
            pe.wait_ge(inner_ready, s + 1)
            if not (isinstance(s, int) and s == 0):
                pe.wait_ge(active_ready, s * IC)
            for c in range(IC):
                last = pe.transpose(upT[:, c * P:(c + 1) * P], inner[:, k % 2, c * P:(c + 1) * P], ident[:, :])
            last.then_inc(upT_full, 1)

        turn(0, 0)
        steps(pe, body)
        second(SLOTS - 1, SLOTS - 1)


_OUT = (B, N, D)


def kernel(**inputs):
    import numpy as _np
    import concourse.bacc as _bacc
    from concourse.bass_utils import run_bass_kernel_spmd as _run

    a = {k: _np.asarray(v) for k, v in inputs.items()}
    x = a["L0_attn_x"]

    def by_row(w):
        return w.T.reshape(KD, P, w.shape[0]).transpose(1, 0, 2)

    wqk = _np.stack([by_row(a[n]) for n in ("L0_attn_Wq", "L0_attn_Wk", "L0_attn_Wk_enc")], 1).reshape(P, 3, KD * D)
    wv = _np.stack([by_row(a[n]) for n in ("L0_attn_Wv", "L0_attn_Wv_enc")], 1).reshape(P, 2 * KD, I)
    arrays = {
        "xT": x.transpose(0, 2, 1).reshape(B, KD, P, N).transpose(0, 2, 1, 3),
        "x": x.reshape(B, NT, P, D).transpose(0, 2, 1, 3),
        "wqk": wqk,
        "wv": wv,
        "wo": a["L0_attn_Wout"].T.reshape(PAIRS, P, D).transpose(1, 0, 2),
        "w1": a["L0_ffn_w1"].reshape(E, KD, P, I).transpose(2, 0, 1, 3),
        "b1": a["L0_ffn_b1"].reshape(E * IC, P).T,
        "w2": a["L0_ffn_w2"].reshape(E, IC, P, D).transpose(2, 0, 1, 3),
        "b2": a["L0_ffn_b2"].reshape(E * D),
        "wr": a["L0_ffn_wr"].reshape(KD, P, E).transpose(1, 0, 2),
        "br": a["L0_ffn_br"],
    }
    arrays = {f"in_{k}": _np.ascontiguousarray(v) for k, v in arrays.items()}
    nc = _bacc.Bacc("TRN2", target_bir_lowering=False, num_devices=1)
    args = [nc.dram_tensor(k, v.shape, mybir.dt.from_np(v.dtype), kind="ExternalInput").ap() for k, v in arrays.items()]
    out = nc.dram_tensor("out", _OUT, F32, kind="ExternalOutput").ap()
    attention_and_experts(nc, *args, out.rearrange("b n d -> (b n) d"))
    r = _run(nc, [arrays], core_ids=[0])
    return r.results[0]["out"]
```
